# Optimizing a Trainium2 kernel written in Bass

```python
import numpy as np
import jax
import jax.numpy as jnp

def _softmax(x, axis=-1):
    return jax.nn.softmax(x, axis=axis)

def _gelu(x):
    return jax.nn.gelu(x, approximate=True)

def _silu(x):
    return jax.nn.silu(x)

def _sigmoid(x):
    return jax.nn.sigmoid(x)

def _layernorm(x, axis=-1, eps=1e-05):
    m = jnp.mean(x, axis=axis, keepdims=True)
    v = jnp.var(x, axis=axis, keepdims=True)
    return (x - m) / jnp.sqrt(v + eps)

def _scatter_add(tgt, idx, src, axis=0):
    return tgt.at[idx].add(src)

def _segment_sum(src, seg, n):
    return jax.ops.segment_sum(src, seg, n)
kernel_name = 'mk_xattn_ffn_d1_seqx_r4_4ec89c'

def setup_inputs(seed: int=0):
    np.random.seed(seed)
    _w = jnp.asarray

    def _rec_inputs():
        import jax
        import jax.numpy as jnp
        _rk = jax.random.key(seed)
        x = 7.22e-05 + 1 * jax.random.normal(jax.random.fold_in(_rk, 1), (16, 128, 256), jnp.float32)
        _lenS = 128 - jax.random.randint(jax.random.fold_in(_rk, 7), (16,), 0, max(1, 128 // 4) + 1, jnp.int32)
        _lenS2 = 128 - jax.random.randint(jax.random.fold_in(_rk, 8), (16,), 0, max(1, 128 // 4) + 1, jnp.int32)
        _ctx_1024P = jax.random.normal(jax.random.fold_in(_rk, 11), (16, 16, 256), jnp.float32)
        _ctx_1024c = jax.random.dirichlet(jax.random.fold_in(_rk, 511), 0.3 * jnp.ones((16,), jnp.float32), (16, 128))
        _ctx_1024t = jnp.einsum('bsk,bkd->bsd', _ctx_1024c, _ctx_1024P)
        _ctx_1024t = _ctx_1024t * jax.lax.rsqrt(jnp.mean(jnp.square(_ctx_1024t)) + 1e-12) * 0.953939
        ctx_1024 = 0.00191187 + 0.999416 * (_ctx_1024t + 0.3 * jax.random.normal(jax.random.fold_in(_rk, 611), (16, 128, 256), jnp.float32))
        return (x, ctx_1024)
    x, ctx_1024 = _rec_inputs()

    def _L0_xattn_setup():
        import jax, jax.numpy as jnp
        import numpy as np
        EPS = 1e-06

        def _rmsnorm(x, w, eps=EPS):
            x32 = x.astype(jnp.float32)
            var = jnp.mean(x32 * x32, axis=-1, keepdims=True)
            return (x32 * jax.lax.rsqrt(var + eps)).astype(x.dtype) * w
        key = jax.random.key(seed)
        ks = jax.random.split(key, 6)
        B, S, K, H = (4, 512, 64, 256)
        return {'hidden_states': jax.random.normal(ks[0], (B, S, H), jnp.float32), 'memory_state': jax.random.normal(ks[1], (B, K, H), jnp.float32), 'q_w': jax.random.normal(ks[2], (H, H), jnp.float32) * (1.0 / np.sqrt(H)), 'k_w': jax.random.normal(ks[3], (H, H), jnp.float32) * (1.0 / np.sqrt(H)), 'norm_w': jnp.ones((H,), jnp.float32), 'gate_w': jax.random.normal(ks[4], (H, H), jnp.float32) * 0.02, 'gate_b': jnp.zeros((H,), jnp.float32)}
    _L0_xattn_all = _L0_xattn_setup()
    _L0_xattn_in = {k: v for k, v in _L0_xattn_all.items() if k in ('q_w', 'k_w', 'norm_w', 'gate_w', 'gate_b')}
    del _L0_xattn_all

    def _L0_ffn_setup():
        import jax, jax.numpy as jnp
        import numpy as np
        S, B, D, E, C, FF = (512, 4, 256, 8, 512, 1024)
        N = S * B
        key = jax.random.key(seed)
        ks = jax.random.split(key, 7)
        return {'hidden_states': jax.random.normal(ks[0], (S, B, D), dtype=jnp.float32), 'combine_weights': jax.random.uniform(ks[1], (N, E), dtype=jnp.float32), 'top_idx': jax.random.randint(ks[2], (C, E), 0, N, dtype=jnp.int64), 'W1': jax.random.normal(ks[3], (E, D, FF), dtype=jnp.float32) * (1.0 / np.sqrt(D)), 'b1': jnp.zeros((E, FF), dtype=jnp.float32), 'W2': jax.random.normal(ks[4], (E, FF, D), dtype=jnp.float32) * (1.0 / np.sqrt(FF)), 'b2': jnp.zeros((E, D), dtype=jnp.float32)}
    _L0_ffn_all = _L0_ffn_setup()
    _L0_ffn_in = {k: v for k, v in _L0_ffn_all.items() if k in ('combine_weights', 'top_idx', 'W1', 'b1', 'W2', 'b2')}
    del _L0_ffn_all
    return {'x': x, 'ctx_1024': ctx_1024, 'L0_xattn_q_w': _L0_xattn_in['q_w'], 'L0_xattn_k_w': _L0_xattn_in['k_w'], 'L0_xattn_norm_w': _L0_xattn_in['norm_w'], 'L0_xattn_gate_w': _L0_xattn_in['gate_w'], 'L0_xattn_gate_b': _L0_xattn_in['gate_b'], 'L0_ffn_combine_weights': _L0_ffn_in['combine_weights'], 'L0_ffn_top_idx': _L0_ffn_in['top_idx'], 'L0_ffn_W1': _L0_ffn_in['W1'], 'L0_ffn_b1': _L0_ffn_in['b1'], 'L0_ffn_W2': _L0_ffn_in['W2'], 'L0_ffn_b2': _L0_ffn_in['b2']}

def reference(x, ctx_1024, L0_xattn_q_w, L0_xattn_k_w, L0_xattn_norm_w, L0_xattn_gate_w, L0_xattn_gate_b, L0_ffn_combine_weights, L0_ffn_top_idx, L0_ffn_W1, L0_ffn_b1, L0_ffn_W2, L0_ffn_b2):
    import jax
    import jax.numpy as jnp

    def _L0_xattn_ref(hidden_states, memory_state, q_w, k_w, norm_w, gate_w, gate_b):
        import jax, jax.numpy as jnp
        import numpy as np
        EPS = 1e-06

        def _rmsnorm(x, w, eps=EPS):
            x32 = x.astype(jnp.float32)
            var = jnp.mean(x32 * x32, axis=-1, keepdims=True)
            return (x32 * jax.lax.rsqrt(var + eps)).astype(x.dtype) * w
        B, S, H = hidden_states.shape
        K = memory_state.shape[1]
        scale = 1.0 / np.sqrt(H)
        normed = _rmsnorm(hidden_states, norm_w)
        v_pool = jnp.concatenate([normed, memory_state], axis=1)
        q = jnp.einsum('bsh,oh->bso', normed, q_w)
        k = jnp.einsum('bth,oh->bto', v_pool, k_w)
        logits = jnp.einsum('bsd,btd->bst', q, k) * scale
        local = jnp.tril(jnp.ones((S, S), bool))
        mask = jnp.concatenate([local, jnp.ones((S, K), bool)], axis=1)
        logits = jnp.where(mask[None], logits, -jnp.inf)
        attn = jax.nn.softmax(logits, axis=-1)
        h_tilde = jnp.einsum('bst,bth->bsh', attn, v_pool)
        alpha = jax.nn.sigmoid(jnp.einsum('bsh,oh->bso', hidden_states, gate_w) + gate_b)
        return (1.0 - alpha) * hidden_states + alpha * h_tilde

    def _L0_ffn_ref(hidden_states, combine_weights, top_idx, W1, b1, W2, b2):
        import jax, jax.numpy as jnp
        import numpy as np
        S, B, D, E, C, FF = (512, 4, 256, 8, 512, 1024)
        N = S * B
        s, b, d = hidden_states.shape
        x = hidden_states.reshape(-1, d)
        tok = top_idx.T
        gathered = x[tok]
        h = jax.nn.gelu(jnp.einsum('ecd,edf->ecf', gathered, W1) + b1[:, None, :])
        out_e = jnp.einsum('ecf,efd->ecd', h, W2) + b2[:, None, :]
        e_ids = jnp.arange(tok.shape[0])[:, None]
        w = combine_weights[tok, e_ids]
        weighted = (out_e * w[..., None]).reshape(-1, d)
        out = jnp.zeros_like(x).at[tok.reshape(-1)].add(weighted)
        return out.reshape(s, b, d)
    x = x + _L0_xattn_ref(_layernorm(x, axis=-1), ctx_1024, L0_xattn_q_w, L0_xattn_k_w, L0_xattn_norm_w, L0_xattn_gate_w, L0_xattn_gate_b)
    x = x + _L0_ffn_ref(_layernorm(x, axis=-1), L0_ffn_combine_weights, L0_ffn_top_idx, L0_ffn_W1, L0_ffn_b1, L0_ffn_W2, L0_ffn_b2)
    return x

_drawn_inputs = setup_inputs


def setup_inputs(seed=0):
    import zlib

    import numpy as np

    out = dict(_drawn_inputs(seed))
    spreads = {'L0_xattn_norm_w': (1.0, 0.6),
     'L0_xattn_gate_b': (0.0, 0.47),
     'L0_ffn_b1': (0.0, 0.1),
     'L0_ffn_b2': (0.0, 0.1)}
    factors = {}
    for name, (base, spread) in spreads.items():
        noise = np.random.default_rng([zlib.crc32(name.encode()), seed]).standard_normal(out[name].shape)
        drawn = base * np.exp(spread * noise) if base else spread * noise
        out[name] = jnp.asarray(drawn.astype(out[name].dtype))
    for name, factor in factors.items():
        out[name] = (out[name] * factor).astype(out[name].dtype)
    return out
```

```python
import concourse.bass as bass
from concourse import mybir
from contextlib import ExitStack


def build_xattn_moe(nc, x_in, ctx_in, q_w, k_w, norm_w, gate_w, gate_b, comb_w, top_idx, W1, b1, W2, b2, out):
    F32, F32R, BF16, I32, U32 = (mybir.dt.float32, mybir.dt.float32r, mybir.dt.bfloat16,
                                 mybir.dt.int32, mybir.dt.uint32)
    ALU, ACT = mybir.AluOpType, mybir.ActivationFunctionType
    ds = bass.ds

    P = 128
    NB, S, H = x_in.shape
    N = NB * S
    KH = H // P
    NPAIR = NB // 2
    SCALE = float(H) ** -0.5
    C, NE = top_idx.shape
    FF = W1.shape[2]
    NF = FF // P
    NT = C // P
    ROW = H + NE
    LN_EPS, RMS_EPS = 1e-5, 1e-6
    PIECE = 512
    W1C = KH * FF
    WC = W1C + NF * H
    NCH = 4
    CH = WC // NCH
    DUP = 1024.0
    SKIP = 4096.0
    MASKED = -1e30

    ctx = ExitStack()
    with ctx:
        def sb(name, shape, dt=F32):
            return ctx.enter_context(nc.sbuf_tensor(name, shape, dt))

        def sem(name):
            return ctx.enter_context(nc.semaphore(name))

        rows_dram = nc.dram_tensor("token_rows", [N, ROW], F32, kind="Internal").ap()

        ident = sb("ident", [P, P])
        causal = sb("causal", [P, 2 * S])
        norm_w_bc = sb("norm_w_bc", [P, H])
        gate_b_bc = sb("gate_b_bc", [P, 2 * H])
        Mqk = sb("Mqk", [P, KH, H])
        gateT = sb("gateT", [P, KH, H])
        bias_rows = sb("bias_rows", [NE * NF + NE * KH, P])
        biasT = sb("biasT", [P, NE * NF + NE * KH])
        wts = sb("wts", [P, 3, KH, H])
        x_all = sb("x_all", [P, NB * H])
        ctx_all = sb("ctx_all", [P, NB * H])
        idx_all = sb("idx_all", [P, NT, NE], I32)
        idx_f = sb("idx_f", [P, NT * NE])
        x3 = x_all[:, :].rearrange("p (b h) -> p b h", h=H)
        c3 = ctx_all[:, :].rearrange("p (b h) -> p b h", h=H)

        bn6 = sb("bn6", [P, NB, 6])
        mv = sb("mv", [P, NB, 2])
        pow_in = sb("pow_in", [P, 2, NB])
        pow_out = sb("pow_out", [P, 2, NB])
        half_neg = sb("half_neg", [P, 2, NB])
        rms_t = sb("rms_t", [P, NB])
        rms_r = sb("rms_r", [P, NB])

        h = sb("h", [P, 2, 2, H])
        pool_nat = sb("pool_nat", [P, 2 * 2 * 2 * H])
        vp = pool_nat[:, :].rearrange("p (s b v h) -> p s b v h", s=2, b=2, v=2)
        keysT = sb("keysT", [P, 2, KH, 2 * S])
        hT = sb("hT", [P, 2, KH, 2 * S])
        qT = sb("qT", [P, KH, 2 * S])
        probs = sb("probs", [P, 2, 2 * S])
        probsT = sb("probsT", [P, 2, 2, S])
        gate_t = sb("gate_t", [P, 2 * H])
        diff = sb("diff", [P, 2, H])
        x_plus_h = sb("x_plus_h", [P, 2, 2 * H])
        x2 = sb("x2", [P, 2, 2, H])
        xn2 = sb("xn2", [P, 2, 2, H])
        mx = sb("mx", [P, 2])
        neg_mx = sb("neg_mx", [P, 2])
        rsum = sb("rsum", [P, 2])
        rinv = sb("rinv", [P, 2])
        bn6b = sb("bn6b", [P, 2, 6])
        mv2 = sb("mv2", [P, 2, 2, 2])
        var_eps = sb("var_eps", [P, 2, 2])
        rstd2 = sb("rstd2", [P, 2, 2])

        w_raw = sb("w_raw", [P, WC])
        w_hi = sb("w_hi", [P, 2, WC], F32R)
        w_lo = sb("w_lo", [P, 2, WC], F32R)
        x_hi = sb("x_hi", [P, 2, KH, C], F32R)
        x_lo = sb("x_lo", [P, 2, KH, C], F32R)
        g32 = sb("g32", [P, 2, C])
        g_hi = sb("g_hi", [P, 2, C], F32R)
        g_lo = sb("g_lo", [P, 2, C], F32R)
        seen = sb("seen", [P, NT, C], BF16)
        junk = sb("junk", [P, C], BF16)
        total = sb("total", [P, NT])
        factor = sb("factor", [P, NT])
        skip_f = sb("skip_f", [P, NT])
        gidx = sb("gidx", [P, 2, NT], I32)
        sidx = sb("sidx", [P, NT], I32)

        xg = x_all[:, 0:2 * NT * ROW].rearrange("p (s t r) -> p s t r", s=2, t=NT)
        accg = x_all[:, 2 * NT * ROW:2 * NT * ROW + NT * H].rearrange("p (t h) -> p t h", h=H)
        idx_rows = ctx_all[:, :].bitcast(I32)
        outT = pool_nat[:, 0:KH * C].rearrange("p (k c) -> p k c", k=KH)
        newrow = pool_nat[:, KH * C:KH * C + NT * H].rearrange("p (t h) -> p t h", h=H)

        banks = [ctx.enter_context(nc.psum_tensor(f"bank{i}", [P, 512], F32)) for i in range(8)]
        ps_keys = [banks[i][:, :].rearrange("p (k t) -> p k t", k=KH) for i in (0, 1)]
        ps_hT = banks[2][:, :].rearrange("p (k t) -> p k t", k=KH)
        ps_q = banks[3][:, :].rearrange("p (k t) -> p k t", k=KH)
        ps_log = banks[4][:, :].rearrange("p (b t) -> p b t", b=2)
        ps_gate = banks[5][:, :].rearrange("p (b t) -> p b t", b=2)
        ps_pT = banks[6][:, :].rearrange("p (b j s) -> p b j s", b=2, j=2)
        ps_pv = banks[7][:, :].rearrange("p (b t) -> p b t", b=2)
        ps_up = banks[0:2]
        ps_down = banks[2:4]
        ps_xT = banks[4:6]
        ps_back = [b[:, :].rearrange("p (t h) -> p t h", h=H) for b in banks[6:8]]

        x_in_s = [sem(f"x_loaded{g}") for g in range(4)]
        c_in_s = [sem(f"ctx_loaded{g}") for g in range(4)]
        wts_in = sem("wts_loaded")
        bc_in = sem("broadcasts_loaded")
        bias_in = sem("bias_loaded")
        idx_in = sem("idx_loaded")
        idxrows_in = sem("idx_rows_loaded")
        comb_in = sem("combine_copied")
        w_in = [sem(f"w_chunk_loaded{c}") for c in range(NCH)]
        consts = sem("pool_constants")
        ident_rdy = sem("ident_ready")
        setup_mm = sem("setup_products")
        setup_ev = sem("setup_evacuated")
        idx_rdy = sem("idx_float_ready")
        st_x = sem("x_stats")
        pow_rdy = sem("x_pow_done")
        rms_rdy = sem("x_rms_steps")
        h_rdy = sem("h_ready")
        n_rdy = sem("normed_ready")
        cv_rdy = sem("context_in_pool")
        keysT_mm = sem("keys_transposed")
        hT_mm = sem("h_transposed")
        keysT_ev = sem("keysT_ready")
        hT_ev = sem("hT_ready")
        q_mm = sem("query_product")
        q_ev = sem("qT_ready")
        log_mm = sem("logits_product")
        log_rdy = sem("masked_logits_max")
        neg_rdy = sem("neg_max_ready")
        exp_rdy = sem("exp_done")
        pT_mm = sem("probs_transposed")
        pT_ev = sem("probsT_ready")
        gate_mm = sem("gate_product")
        gate_rdy = sem("gate_logit_ready")
        tanh_rdy = sem("tanh_done")
        pv_mm = sem("values_product")
        ri_rdy = sem("inverse_sum_ready")
        diff_rdy = sem("diff_ready")
        mix_rdy = sem("mixed_ready")
        xh_rdy = sem("x_plus_h_ready")
        x2_rdy = sem("x2_ready")
        st2 = sem("x2_stats")
        ve_rdy = sem("x2_var_eps_ready")
        rstd_rdy = sem("x2_rstd_ready")
        xn_rdy = sem("xn2_ready")
        x2_out = [sem(f"x2_stored{s}") for s in range(2)]
        xn_out = [sem(f"xn2_stored{s}") for s in range(2)]
        whi_rdy = sem("w_hi_ready")
        wlo_rdy = sem("w_lo_ready")
        gidx_rdy = sem("gather_idx_ready")
        xg_in = [sem(f"rows_gathered{s}") for s in range(2)]
        acc_in = sem("sums_gathered")
        scat = sem("sums_scattered")
        xT_mm = sem("rows_transposed")
        xhi_rdy = sem("x_hi_ready")
        xlo_rdy = sem("x_lo_ready")
        up_mm = sem("up_product")
        g_rdy = sem("gelu_done")
        glo_rdy = sem("g_lo_ready")
        down_mm = sem("down_product")
        oT_act = sem("outT_tile0_ready")
        oT_dve = sem("outT_tile1_ready")
        back_mm = sem("out_transposed_back")
        new_rdy = sem("new_sums_ready")
        tot_rdy = sem("slot_totals")
        skip_rdy = sem("skip_ready")
        fac_rdy = sem("factor_ready")
        sidx_rdy = sem("scatter_idx_ready")

        waits_taken = sem("waits_taken")

        block = ctx.enter_context(nc.Block())

        def take_waits(eng):
            eng.sem_inc(waits_taken, 1)

        def each_item(eng, body):
            body(0, 0, 0)
            with eng.Fori(0, 3) as i:
                body(2 * i + 1, 1, i)
                body(2 * i + 2, 0, i + 1)
            body(7, 1, 3)

        def is_first(item):
            return isinstance(item, int) and item == 0

        def is_last(item):
            return isinstance(item, int) and item == 7

        def w_chunk(e, c):
            if c < KH:
                return W1[ds(e, 1), c * P:(c + 1) * P, :].rearrange("e p f -> p (e f)")
            t = NF // (NCH - KH)
            return W2[ds(e, 1), (c - KH) * t * P:(c - KH + 1) * t * P, :].rearrange("e (f p) d -> p (e f) d", p=P)

        def w_chunk_dst(c):
            dst = w_raw[:, c * CH:(c + 1) * CH]
            return dst if c < KH else dst.rearrange("p (f d) -> p f d", d=H)

        @block.sync
        def _(sp):
            x_v = x_in.rearrange("b s h -> s b h")
            c_v = ctx_in.rearrange("b s h -> s b h")
            q = NB // 4
            sp.dma_start(x3[:, 0:q, :], x_v[:, 0:q, :]).then_inc(x_in_s[0], 16)
            for n, w in enumerate((q_w, k_w, gate_w)):
                sp.dma_start(wts[:, n, :, :], w.rearrange("(k p) h -> p k h", p=P)).then_inc(wts_in, 16)
            sp.dma_start(norm_w_bc[:, :], norm_w.rearrange("(a h) -> a h", a=1).broadcast_to([P, H])).then_inc(bc_in, 16)
            for n in range(2):
                sp.dma_start(gate_b_bc[:, n * H:(n + 1) * H],
                             gate_b.rearrange("(a h) -> a h", a=1).broadcast_to([P, H])).then_inc(bc_in, 16)
            sp.dma_start(c3[:, 0:q, :], c_v[:, 0:q, :]).then_inc(c_in_s[0], 16)
            for g in range(1, 4):
                sp.dma_start(x3[:, g * q:(g + 1) * q, :], x_v[:, g * q:(g + 1) * q, :]).then_inc(x_in_s[g], 16)
                sp.dma_start(c3[:, g * q:(g + 1) * q, :], c_v[:, g * q:(g + 1) * q, :]).then_inc(c_in_s[g], 16)
            sp.dma_start(bias_rows[0:NE * NF, :], b1.rearrange("e (f p) -> (e f) p", p=P)).then_inc(bias_in, 16)
            sp.dma_start(bias_rows[NE * NF:, :], b2.rearrange("e (k p) -> (e k) p", p=P)).then_inc(bias_in, 16)
            sp.dma_start(idx_all[:, :, :], top_idx.rearrange("(p t) e -> p t e", t=NT)).then_inc(idx_in, 16)
            for c in range(NCH):
                sp.dma_start(w_chunk_dst(c), w_chunk(0, c)).then_inc(w_in[c], 16)
            sp.dma_start(rows_dram[:, H:ROW], comb_w).then_inc(comb_in, 16)
            out_v = out.rearrange("b s h -> s b h")
            rows_v = rows_dram.rearrange("(b s) r -> s b r", s=S)
            for r in range(NPAIR):
                sp.wait_ge(x2_rdy, r + 1)
                sp.dma_start(out_v[:, 2 * r:2 * r + 2, :], x2[:, r % 2, :, :]).then_inc(x2_out[r % 2], 16)
                sp.wait_ge(xn_rdy, 2 * r + 2)
                sp.dma_start(rows_v[:, 2 * r:2 * r + 2, 0:H], xn2[:, r % 2, :, :]).then_inc(xn_out[r % 2], 16)
                if r % 2 == 1:
                    sp.wait_ge(wlo_rdy, r + 1)
                    sp.dma_start(w_chunk_dst(r // 2), w_chunk(1, r // 2)).then_inc(w_in[r // 2], 16)
            sp.wait_ge(cv_rdy, NPAIR)
            sp.dma_start(idx_rows[:, :], top_idx.rearrange("(a c) e -> a (c e)", a=1).broadcast_to([P, C * NE]))\
                .then_inc(idxrows_in, 16)
            with sp.Fori(2, NE) as e:
                for c in range(NCH):
                    sp.wait_ge(wlo_rdy, 8 * e - 8 + 2 * c + 2)
                    sp.dma_start(w_chunk_dst(c), w_chunk(e, c)).then_inc(w_in[c], 16)

        @block.gpsimd
        def _(pool):
            g = nc.gpsimd
            g.memset(ident[:, :], 0.0).then_inc(consts, 1)
            g.memset(half_neg[:, :, :], -0.5).then_inc(consts, 1)
            g.memset(causal[:, :], 0.0).then_inc(consts, 1)
            g.memset(seen[:, :, :], 1.0).then_inc(consts, 1)
            pool.wait_ge(consts, 4)
            g.affine_select(out=ident[:, :], in_=ident[:, :], compare_op=ALU.not_equal, fill=1.0, base=0,
                            pattern=[[-1, P]], channel_multiplier=1).then_inc(ident_rdy, 1)
            g.affine_select(out=causal[:, 0:S], in_=causal[:, 0:S], compare_op=ALU.is_ge, fill=MASKED, base=0,
                            pattern=[[-1, S]], channel_multiplier=1).then_inc(ident_rdy, 1)

            def x_powers(b0, b1_, n):
                pool.wait_ge(st_x, n)
                g.tensor_tensor(pow_out[:, :, b0:b1_], pow_in[:, :, b0:b1_], half_neg[:, :, b0:b1_], ALU.pow)\
                    .then_inc(pow_rdy, 1)

            def context_to_pool(p, s):
                g.tensor_copy(vp[:, s, :, 1, :], c3[:, ds(2 * p, 2), :]).then_inc(cv_rdy, 1)

            x_powers(0, 4, 1)
            pool.wait_ge(c_in_s[0], 16)
            context_to_pool(0, 0)
            x_powers(4, NB, 2)
            for t in range(NT):
                g.affine_select(out=seen[:, t, :], in_=seen[:, t, :], compare_op=ALU.is_ge, fill=DUP, base=-t,
                                pattern=[[1, C]], channel_multiplier=-NT).then_inc(consts, 1)
            for q in range(1, 4):
                pool.wait_ge(c_in_s[q], 16)

            def normalise(r, s, use):
                pool.wait_ge(xn_out[s], 16 * use + 16)
                pool.wait_ge(ve_rdy, r + 1)
                g.tensor_tensor(rstd2[:, s, :], var_eps[:, s, :], half_neg[:, 0, 0:2], ALU.pow).then_inc(rstd_rdy, 1)
                pool.wait_ge(rstd_rdy, r + 1)
                take_waits(pool)
                for b in range(2):
                    g.tensor_scalar(xn2[:, s, b, :], x2[:, s, b, :], mv2[:, s, b, 0:1], rstd2[:, s, b:b + 1],
                                    ALU.subtract, ALU.mult).then_inc(xn_rdy, 1)

            def attention(p, s, use):
                if not is_last(p):
                    if not is_first(p):
                        pool.wait_ge(pv_mm, p)
                    context_to_pool(p + 1, 1 - s)
                pool.wait_ge(h_rdy, 2 * p + 2)
                g.tensor_tensor(x_plus_h[:, s, :], x_all[:, ds(p * (2 * H), 2 * H)],
                                h[:, s, :, :].rearrange("p b h -> p (b h)"), ALU.add).then_inc(xh_rdy, 1)
                if not is_first(p):
                    normalise(p - 1, 1 - s, use if s == 1 else use - 1)

            each_item(pool, attention)
            normalise(7, 1, 3)

            idx = bass.IndirectOffsetOnAxis
            flat = out.rearrange("b s h -> (b s) h")

            def gather_rows(s):
                take_waits(pool)
                for t in range(NT):
                    g.indirect_dma_start(xg[:, s, t, :], None, rows_dram, idx(gidx[:, s, t:t + 1].bitcast(U32), 0))\
                        .then_inc(xg_in[s], 16)

            def gather_sums(s):
                take_waits(pool)
                for t in range(NT):
                    g.indirect_dma_start(accg[:, t, :], None, flat, idx(gidx[:, s, t:t + 1].bitcast(U32), 0))\
                        .then_inc(acc_in, 16)

            def scatter_sums():
                take_waits(pool)
                for t in range(NT):
                    g.indirect_dma_start(flat, idx(sidx[:, t:t + 1].bitcast(U32), 0), newrow[:, t, :], None,
                                         bounds_check=N - 1, oob_is_err=False).then_inc(scat, 16)

            pool.wait_ge(comb_in, 16)
            for s in range(2):
                pool.wait_ge(xn_out[s], 16 * (NPAIR // 2) + 16)
                pool.wait_ge(x2_out[s], 16 * (NPAIR // 2) + 16)
            pool.wait_ge(gidx_rdy, 1)
            gather_rows(0)

            def expert(e, s, use):
                if not is_last(e):
                    pool.wait_ge(gidx_rdy, e + 2)
                    gather_rows(1 - s)
                if not is_first(e):
                    pool.wait_ge(new_rdy, NT * e)
                    scatter_sums()
                    pool.wait_ge(scat, 16 * NT * e)
                gather_sums(s)

            each_item(pool, expert)
            pool.wait_ge(new_rdy, NT * NE)
            scatter_sums()
            pool.wait_ge(scat, 16 * NT * NE)

        @block.scalar
        def _(act):
            a = nc.scalar
            for s in range(2):
                act.sem_inc(x2_out[s], 16)
                act.sem_inc(xn_out[s], 16)
            act.wait_ge(setup_mm, 1)
            a.copy(Mqk[:, :, :], ps_log).then_inc(setup_ev, 1)
            act.wait_ge(setup_mm, 2)
            a.copy(gateT[:, :, :], ps_gate).then_inc(setup_ev, 1)

            def keys(p, b):
                act.wait_ge(keysT_mm, 2 * p + b + 1)
                a.copy(keysT[:, b, :, :], ps_keys[b]).then_inc(keysT_ev, 1)

            def h_transposed(p, s):
                act.wait_ge(hT_mm, p + 1)
                a.copy(hT[:, s, :, :], ps_hT).then_inc(hT_ev, 1)

            def query(p):
                act.wait_ge(q_mm, p + 1)
                a.copy(qT[:, :, :], ps_q).then_inc(q_ev, 1)

            def split_hi(piece_count, col, s, e_loaded, c):
                act.wait_ge(w_in[c], e_loaded)
                a.copy(w_hi[:, s, col], w_raw[:, col]).then_inc(whi_rdy, 1)

            keys(0, 0)
            keys(0, 1)
            h_transposed(0, 0)
            query(0)
            act.wait_ge(setup_mm, 3)
            a.copy(biasT[:, :], ps_pv.rearrange("p b t -> p (b t)")[:, 0:NE * NF + NE * KH]).then_inc(setup_ev, 1)
            for c in range(NCH):
                act.wait_ge(w_in[c], 16)

            def attention(p, s, use):
                if not is_last(p):
                    keys(p + 1, 0)
                for b in range(2):
                    act.wait_ge(neg_rdy, 2 * p + b + 1)
                    a.activation(probs[:, b, :], probs[:, b, :], ACT.Exp, bias=neg_mx[:, b:b + 1], scale=SCALE,
                                 accum_out=rsum[:, b:b + 1]).then_inc(exp_rdy, 1)
                if not is_last(p):
                    keys(p + 1, 1)
                act.wait_ge(pT_mm, p + 1)
                a.copy(probsT[:, :, :, :], ps_pT).then_inc(pT_ev, 1)
                if not is_last(p):
                    h_transposed(p + 1, 1 - s)
                act.wait_ge(gate_rdy, p + 1)
                a.activation(gate_t[:, :], gate_t[:, :], ACT.Tanh, scale=0.5).then_inc(tanh_rdy, 1)
                if not is_last(p):
                    query(p + 1)
                col = ds(p * PIECE, PIECE)
                a.copy(w_hi[:, 0, col], w_raw[:, col]).then_inc(whi_rdy, 1)

            each_item(act, attention)

            def x_hi_part(e, s):
                for k in range(KH):
                    act.wait_ge(xT_mm, KH * e + k + 1)
                    a.copy(x_hi[:, s, k, :], ps_xT[k][:, :]).then_inc(xhi_rdy, 1)

            def out_tile0(e):
                act.wait_ge(down_mm, NF * e + NF)
                a.activation(outT[:, 0, :], ps_down[0][:, :], ACT.Identity,
                             bias=biasT[:, ds(NE * NF + e * KH, 1)]).then_inc(oT_act, 1)

            x_hi_part(0, 0)

            def expert(e, s, use):
                for f in range(NF):
                    act.wait_ge(up_mm, NF * e + f + 1)
                    bias = biasT[:, ds(e * NF + f, 1)]
                    a.activation(g32[:, f % 2, :], ps_up[f % 2][:, :], ACT.Gelu_apprx_tanh, bias=bias)
                    a.activation(g_hi[:, f % 2, :], ps_up[f % 2][:, :], ACT.Gelu_apprx_tanh, bias=bias)\
                        .then_inc(g_rdy, 1)
                    if f == 0 and not is_first(e):
                        out_tile0(e - 1)
                    if not is_last(e):
                        if f % 2 == 0:
                            act.wait_ge(w_in[f // 2], 16 * e + 32)
                        col = slice(f * PIECE, (f + 1) * PIECE)
                        a.copy(w_hi[:, 1 - s, col], w_raw[:, col]).then_inc(whi_rdy, 1)
                        if f == 4:
                            x_hi_part(e + 1, 1 - s)

            each_item(act, expert)
            out_tile0(7)

        @block.vector
        def _(dve):
            v = nc.vector

            def x_stats(b0, b1_, n):
                for b in range(b0, b1_):
                    if b % 4 == 0:
                        dve.wait_ge(x_in_s[b // 4], 16)
                    v.bn_stats(bn6[:, b, :], x3[:, b, :]).then_inc(rms_rdy, 1)
                dve.wait_ge(rms_rdy, x_steps[0] + b1_ - b0)
                for b in range(b0, b1_):
                    v.bn_aggr(mv[:, b, :], bn6[:, b, :]).then_inc(rms_rdy, 1)
                dve.wait_ge(rms_rdy, x_steps[0] + 2 * (b1_ - b0))
                x_steps[0] += 2 * (b1_ - b0)
                v.tensor_scalar(pow_in[:, 0, b0:b1_], mv[:, b0:b1_, 1], LN_EPS, None, ALU.add)
                v.tensor_scalar(pow_in[:, 1, b0:b1_], mv[:, b0:b1_, 1], 1.0 + RMS_EPS, LN_EPS * RMS_EPS,
                                ALU.mult, ALU.add).then_inc(st_x, 1)

            def x_rms(b0, b1_, n):
                dve.wait_ge(pow_rdy, n)
                v.tensor_tensor(rms_t[:, b0:b1_], pow_in[:, 0, b0:b1_], pow_out[:, 0, b0:b1_], ALU.mult)\
                    .then_inc(rms_rdy, 1)
                dve.wait_ge(rms_rdy, x_steps[0] + 1)
                v.tensor_tensor(rms_r[:, b0:b1_], rms_t[:, b0:b1_], pow_out[:, 1, b0:b1_], ALU.mult)\
                    .then_inc(rms_rdy, 1)
                dve.wait_ge(rms_rdy, x_steps[0] + 2)
                x_steps[0] += 2

            def norms(p, s):
                for b in range(2):
                    if not (is_first(p) or isinstance(p, int) and p == 1):
                        if b == 0:
                            dve.wait_ge(xh_rdy, p - 1)
                        dve.wait_ge(diff_rdy, 2 * p - 4 + b + 1)
                    v.tensor_scalar(h[:, s, b, :], x_all[:, ds((2 * p + b) * H, H)], mv3[:, ds(4 * p + 2 * b, 1)],
                                    pow_out[:, 0, ds(2 * p + b, 1)], ALU.subtract, ALU.mult).then_inc(h_rdy, 1)
                for b in range(2):
                    dve.wait_ge(h_rdy, 2 * p + b + 1)
                    v.scalar_tensor_tensor(vp[:, s, b, 0, :], h[:, s, b, :], rms_r[:, ds(2 * p + b, 1)],
                                           norm_w_bc[:, :], ALU.mult, ALU.mult).then_inc(n_rdy, 1)

            mv3 = mv[:, :, :].rearrange("p b c -> p (b c)")
            x_steps = [0]
            x_stats(0, 4, 0)
            x_rms(0, 4, 1)
            dve.wait_ge(bc_in, 48)
            norms(0, 0)
            dve.wait_ge(idx_in, 16)
            v.tensor_copy(idx_f[:, :], idx_all[:, :, :].rearrange("p t e -> p (t e)")).then_inc(idx_rdy, 1)
            v.tensor_copy(gidx[:, 0, :], idx_all[:, :, 0]).then_inc(gidx_rdy, 1)
            x_stats(4, NB, 1)
            norms(1, 1)
            x_rms(4, NB, 2)
            dve.wait_ge(ident_rdy, 2)

            def finish_diff(p, s):
                for b in range(2):
                    if b == 0:
                        dve.wait_ge(pv_mm, p + 1)
                        dve.wait_ge(ri_rdy, p + 1)
                    v.scalar_tensor_tensor(diff[:, b, :], ps_pv[:, b, :], rinv[:, b:b + 1], h[:, s, b, :],
                                           ALU.mult, ALU.subtract).then_inc(diff_rdy, 1)

            def mix(p):
                dve.wait_ge(tanh_rdy, p + 1)
                dve.wait_ge(diff_rdy, 2 * p + 2)
                d = diff[:, :, :].rearrange("p b h -> p (b h)")
                v.scalar_tensor_tensor(d, gate_t[:, :], 1.0, d, ALU.add, ALU.mult).then_inc(mix_rdy, 1)

            def residual(p, s, use):
                dve.wait_ge(mix_rdy, p + 1)
                dve.wait_ge(xh_rdy, p + 1)
                dve.wait_ge(x2_out[s], 16 * use + 16)
                v.scalar_tensor_tensor(x2[:, s, :, :].rearrange("p b h -> p (b h)"),
                                       diff[:, :, :].rearrange("p b h -> p (b h)"), 0.5, x_plus_h[:, s, :],
                                       ALU.mult, ALU.add).then_inc(x2_rdy, 1)

            def stats2(p, s):
                dve.wait_ge(x2_rdy, p + 1)
                for b in range(2):
                    v.bn_stats(bn6b[:, b, :], x2[:, s, b, :]).then_inc(st2, 1)

            def aggr2(p, s):
                for b in range(2):
                    dve.wait_ge(st2, 4 * p + b + 1)
                    take_waits(dve)
                    v.bn_aggr(mv2[:, s, b, :], bn6b[:, b, :]).then_inc(st2, 1)
                dve.wait_ge(st2, 4 * p + 4)
                v.tensor_scalar(var_eps[:, s, :], mv2[:, s, :, 1], LN_EPS, None, ALU.add).then_inc(ve_rdy, 1)

            def attention(p, s, use):
                last_use = use if s == 1 else use - 1
                if not is_first(p):
                    finish_diff(p - 1, 1 - s)
                    if not is_last(p):
                        norms(p + 1, 1 - s)
                dve.wait_ge(log_mm, p + 1)
                if not is_first(p):
                    dve.wait_ge(pT_mm, p)
                take_waits(dve)
                for b in range(2):
                    v.tensor_tensor_reduce(out=probs[:, b, :], in0=ps_log[:, b, :], in1=causal[:, :], scale=1.0,
                                           scalar=-3.0e38, op0=ALU.add, op1=ALU.max, accum_out=mx[:, b:b + 1])\
                        .then_inc(log_rdy, 1)
                for b in range(2):
                    dve.wait_ge(log_rdy, 2 * p + b + 1)
                    v.tensor_scalar(neg_mx[:, b:b + 1], mx[:, b:b + 1], -SCALE, None, ALU.mult).then_inc(neg_rdy, 1)
                if not is_first(p):
                    mix(p - 1)
                dve.wait_ge(gate_mm, p + 1)
                if not is_first(p):
                    dve.wait_ge(mix_rdy, p)
                v.tensor_tensor(gate_t[:, :], ps_gate.rearrange("p b h -> p (b h)"), gate_b_bc[:, :], ALU.add)\
                    .then_inc(gate_rdy, 1)
                if not is_first(p):
                    residual(p - 1, 1 - s, last_use)
                dve.wait_ge(whi_rdy, p + 1)
                col = ds(p * PIECE, PIECE)
                v.tensor_tensor(w_lo[:, 0, col], w_raw[:, col], w_hi[:, 0, col].bitcast(F32), ALU.subtract)\
                    .then_inc(wlo_rdy, 1)
                if not is_first(p):
                    stats2(p - 1, 1 - s)
                dve.wait_ge(exp_rdy, 2 * p + 2)
                v.reciprocal(rinv[:, :], rsum[:, :]).then_inc(ri_rdy, 1)
                if not is_first(p):
                    aggr2(p - 1, 1 - s)

            each_item(dve, attention)
            finish_diff(7, 1)
            mix(7)
            residual(7, 1, 3)
            stats2(7, 1)
            aggr2(7, 1)

            def x_lo_part(e, s):
                for k in range(KH):
                    dve.wait_ge(xhi_rdy, KH * e + k + 1)
                    v.tensor_tensor(x_lo[:, s, k, :], ps_xT[k][:, :], x_hi[:, s, k, :].bitcast(F32), ALU.subtract)\
                        .then_inc(xlo_rdy, 1)

            def out_tile1(e):
                dve.wait_ge(down_mm, NF * e + NF)
                v.tensor_scalar(outT[:, 1, :], ps_down[1][:, :], biasT[:, ds(NE * NF + e * KH + 1, 1)], None, ALU.add)\
                    .then_inc(oT_dve, 1)

            def new_sums(e):
                dve.wait_ge(acc_in, 16 * NT * (e + 1))
                dve.wait_ge(fac_rdy, e + 1)
                for t in range(NT):
                    if t % 2 == 0:
                        dve.wait_ge(back_mm, NT // 2 * e + t // 2 + 1)
                    v.scalar_tensor_tensor(newrow[:, t, :], ps_back[t // 2][:, t % 2, :], factor[:, t:t + 1],
                                           accg[:, t, :], ALU.mult, ALU.add).then_inc(new_rdy, 1)

            rows_by_expert = idx_rows[:, :].rearrange("p (c e) -> p e c", e=NE)

            def slot_total(e, t):
                v.scalar_tensor_tensor(junk[:, :], rows_by_expert[:, ds(e, 1), :].rearrange("p a c -> p (a c)"),
                                       idx_f[:, ds(t * NE + e, 1)], seen[:, t, :], ALU.is_equal, ALU.mult,
                                       accum_out=total[:, t:t + 1]).then_inc(tot_rdy, 1)

            x_lo_part(0, 0)
            dve.wait_ge(idxrows_in, 16)
            dve.wait_ge(idx_rdy, 1)
            dve.wait_ge(consts, 4 + NT)

            def expert(e, s, use):
                if not is_last(e):
                    if not is_first(e):
                        dve.wait_ge(acc_in, 16 * NT * e)
                    v.tensor_copy(gidx[:, 1 - s, :], idx_all[:, :, ds(e + 1, 1)].rearrange("p t a -> p (t a)"))\
                        .then_inc(gidx_rdy, 1)
                for f in range(NF):
                    dve.wait_ge(g_rdy, NF * e + f + 1)
                    v.tensor_tensor(g_lo[:, f % 2, :], g32[:, f % 2, :], g_hi[:, f % 2, :].bitcast(F32), ALU.subtract)\
                        .then_inc(glo_rdy, 1)
                    if f == 0 and not is_first(e):
                        out_tile1(e - 1)
                    if f == 1 and not is_first(e):
                        new_sums(e - 1)
                    if not is_last(e):
                        col = slice(f * PIECE, (f + 1) * PIECE)
                        dve.wait_ge(whi_rdy, 8 * e + 8 + f + 1)
                        v.tensor_tensor(w_lo[:, 1 - s, col], w_raw[:, col], w_hi[:, 1 - s, col].bitcast(F32),
                                        ALU.subtract).then_inc(wlo_rdy, 1)
                        if f == 5:
                            x_lo_part(e + 1, 1 - s)
                    if f == 2 or f == 3 or f == 4 or f == 6:
                        n = (2, 3, 4, 6).index(f)
                        if not is_first(e):
                            dve.wait_ge(tot_rdy, NT * e + n)
                        elif n:
                            dve.wait_ge(tot_rdy, n)
                        slot_total(e, n)
                    if f == 7:
                        dve.wait_ge(tot_rdy, NT * e + NT)
                        v.tensor_tensor(factor[:, :], total[:, :],
                                        xg[:, s, :, ds(e + H, 1)].rearrange("p t a -> p (t a)"), ALU.mult)\
                            .then_inc(fac_rdy, 1)
                        v.tensor_scalar(skip_f[:, :], total[:, :], DUP, SKIP, ALU.is_ge, ALU.mult).then_inc(skip_rdy, 1)
                        dve.wait_ge(skip_rdy, e + 1)
                        if not is_first(e):
                            dve.wait_ge(scat, 16 * NT * e)
                        v.tensor_tensor(sidx[:, :], skip_f[:, :],
                                        idx_f[:, :].rearrange("p (t e) -> p t e", e=NE)[:, :, ds(e, 1)]
                                        .rearrange("p t a -> p (t a)"), ALU.add).then_inc(sidx_rdy, 1)

            each_item(dve, expert)
            out_tile1(7)
            dve.wait_ge(sidx_rdy, NE)
            new_sums(7)

        @block.tensor
        def _(pe):
            t_ = nc.tensor
            pe.wait_ge(wts_in, 48)
            pe.wait_ge(ident_rdy, 2)
            for m in range(KH):
                for k in range(KH):
                    last = t_.matmul(ps_log[:, m, :], wts[:, 0, k, m * P:(m + 1) * P], wts[:, 1, k, :],
                                     start=(k == 0), stop=(k == KH - 1))
            last.then_inc(setup_mm, 1)
            for k in range(KH):
                for o in range(KH):
                    last = t_.transpose(ps_gate[:, k, o * P:(o + 1) * P], wts[:, 2, o, k * P:(k + 1) * P], ident[:, :])
            last.then_inc(setup_mm, 1)

            def transposes(p, s):
                pe.wait_ge(cv_rdy, p + 1)
                for b in range(2):
                    pe.wait_ge(n_rdy, 2 * p + b + 1)
                    if not is_first(p):
                        pe.wait_ge(keysT_ev, 2 * p - 1 + b)
                    for k in range(KH):
                        for j in range(2):
                            last = t_.transpose(ps_keys[b][:, k, j * S:(j + 1) * S], vp[:, s, b, j, k * P:(k + 1) * P],
                                                ident[:, :])
                    last.then_inc(keysT_mm, 1)
                if not is_first(p):
                    pe.wait_ge(hT_ev, p)
                for k in range(KH):
                    for b in range(2):
                        last = t_.transpose(ps_hT[:, k, b * S:(b + 1) * S], h[:, s, b, k * P:(k + 1) * P], ident[:, :])
                last.then_inc(hT_mm, 1)

            def query(p):
                pe.wait_ge(keysT_ev, 2 * p + 2)
                if not is_first(p):
                    pe.wait_ge(q_ev, p)
                for m in range(KH):
                    for k in range(KH):
                        last = t_.matmul(ps_q[:, m, :].rearrange("p (b t) -> p b t", b=2), Mqk[:, k, m * P:(m + 1) * P],
                                         keysT[:, :, k, 0:S], start=(k == 0), stop=(k == KH - 1))
                last.then_inc(q_mm, 1)

            transposes(0, 0)
            pe.wait_ge(setup_ev, 1)
            query(0)
            pe.wait_ge(bias_in, 32)
            nbias = NE * NF + NE * KH
            t_.transpose(ps_pv.rearrange("p b t -> p (b t)")[:, 0:nbias], bias_rows[:, :], ident[0:nbias, 0:nbias])\
                .then_inc(setup_mm, 1)

            def attention(p, s, use):
                pe.wait_ge(q_ev, p + 1)
                if not is_first(p):
                    pe.wait_ge(log_rdy, 2 * p)
                for b in range(2):
                    for k in range(KH):
                        last = t_.matmul(ps_log[:, b, :], qT[:, k, b * S:(b + 1) * S], keysT[:, b, k, :],
                                         start=(k == 0), stop=(k == KH - 1))
                last.then_inc(log_mm, 1)
                if not is_last(p):
                    transposes(p + 1, 1 - s)
                pe.wait_ge(hT_ev, p + 1)
                if is_first(p):
                    pe.wait_ge(setup_ev, 2)
                else:
                    pe.wait_ge(gate_rdy, p)
                for b in range(2):
                    for k in range(KH):
                        last = t_.matmul(ps_gate[:, b, :], hT[:, s, k, b * S:(b + 1) * S], gateT[:, k, :],
                                         start=(k == 0), stop=(k == KH - 1))
                last.then_inc(gate_mm, 1)
                pe.wait_ge(exp_rdy, 2 * p + 2)
                if not is_first(p):
                    pe.wait_ge(pT_ev, p)
                for b in range(2):
                    for j in range(2):
                        last = t_.transpose(ps_pT[:, b, j, :], probs[:, b, j * S:(j + 1) * S], ident[:, :])
                last.then_inc(pT_mm, 1)
                if not is_last(p):
                    query(p + 1)
                pe.wait_ge(pT_ev, p + 1)
                if is_first(p):
                    pe.wait_ge(setup_ev, 3)
                else:
                    pe.wait_ge(diff_rdy, 2 * p)
                for b in range(2):
                    for j in range(2):
                        last = t_.matmul(ps_pv[:, b, :], probsT[:, b, j, :], vp[:, s, b, j, :],
                                         start=(j == 0), stop=(j == 1))
                last.then_inc(pv_mm, 1)

            each_item(pe, attention)

            def three_passes(dst, lhs_hi, lhs_lo, rhs_hi, rhs_lo, first, last_one):
                t_.matmul(dst, lhs_hi, rhs_hi, start=first, stop=False)
                t_.matmul(dst, lhs_hi, rhs_lo, start=False, stop=False)
                return t_.matmul(dst, lhs_lo, rhs_hi, start=False, stop=last_one)

            def rows_transposed(e, s, use):
                pe.wait_ge(xg_in[s], 16 * NT * (use + 1))
                if not is_first(e):
                    pe.wait_ge(xlo_rdy, KH * e)
                for k in range(KH):
                    for t in range(NT):
                        last = t_.transpose(ps_xT[k][:, t * P:(t + 1) * P], xg[:, s, t, k * P:(k + 1) * P], ident[:, :])
                    last.then_inc(xT_mm, 1)

            def up(e, s, f):
                if f == 0:
                    pe.wait_ge(xlo_rdy, KH * e + KH)
                    pe.wait_ge(wlo_rdy, 8 * e + 8)
                if not (is_first(e) and f < 2):
                    pe.wait_ge(g_rdy, NF * e + f - 1)
                for k in range(KH):
                    c = slice(k * FF + f * P, k * FF + (f + 1) * P)
                    last = three_passes(ps_up[f % 2][:, :], w_hi[:, s, c], w_lo[:, s, c], x_hi[:, s, k, :],
                                        x_lo[:, s, k, :], k == 0, k == KH - 1)
                last.then_inc(up_mm, 1)

            def down(e, s, f):
                if f == 0 and not is_first(e):
                    pe.wait_ge(oT_act, e)
                    pe.wait_ge(oT_dve, e)
                pe.wait_ge(glo_rdy, NF * e + f + 1)
                for m in range(KH):
                    c = slice(W1C + f * H + m * P, W1C + f * H + (m + 1) * P)
                    last = three_passes(ps_down[m][:, :], w_hi[:, s, c], w_lo[:, s, c], g_hi[:, f % 2, :],
                                        g_lo[:, f % 2, :], f == 0, f == NF - 1)
                last.then_inc(down_mm, 1)

            def back(e):
                pe.wait_ge(oT_act, e + 1)
                pe.wait_ge(oT_dve, e + 1)
                for t in range(NT):
                    for m in range(KH):
                        last = t_.transpose(ps_back[t // 2][:, t % 2, m * P:(m + 1) * P], outT[:, m, t * P:(t + 1) * P],
                                            ident[:, :])
                    if t % 2 == 1:
                        last.then_inc(back_mm, 1)

            rows_transposed(0, 0, 0)

            def expert(e, s, use):
                up(e, s, 0)
                if not is_first(e):
                    down(e - 1, 1 - s, NF - 1)
                up(e, s, 1)
                if not is_first(e):
                    back(e - 1)
                down(e, s, 0)
                for f in range(2, NF):
                    if f == 4 and not is_last(e):
                        rows_transposed(e + 1, 1 - s, use if s == 0 else use + 1)
                    up(e, s, f)
                    down(e, s, f - 1)

            each_item(pe, expert)
            down(7, 1, NF - 1)
            back(7)


_INS = ['x', 'ctx_1024', 'L0_xattn_q_w', 'L0_xattn_k_w', 'L0_xattn_norm_w', 'L0_xattn_gate_w', 'L0_xattn_gate_b',
        'L0_ffn_combine_weights', 'L0_ffn_top_idx', 'L0_ffn_W1', 'L0_ffn_b1', 'L0_ffn_W2', 'L0_ffn_b2']


def kernel(**inputs):
    import numpy as _np
    import concourse.bacc as _bacc
    from concourse import mybir as _mybir
    from concourse.bass_utils import run_bass_kernel_spmd as _run

    nc = _bacc.Bacc("TRN2", target_bir_lowering=False, num_devices=1)
    arrays, args = {}, []
    for name in _INS:
        a = _np.ascontiguousarray(inputs[name])
        arrays[f"in_{name}_dram"] = a
        args.append(nc.dram_tensor(f"in_{name}_dram", a.shape, _mybir.dt.from_np(a.dtype), kind="ExternalInput").ap())
    args.append(nc.dram_tensor("out_0_dram", inputs["x"].shape, _mybir.dt.float32, kind="ExternalOutput").ap())
    build_xattn_moe(nc, *args)
    r = _run(nc, [arrays], core_ids=[0])
    return r.results[0]["out_0_dram"]
```

```python
import concourse.bass as bass
from concourse import mybir
from contextlib import ExitStack


def build_xattn_moe(nc, x_in, ctx_in, q_w, k_w, norm_w, gate_w, gate_b, comb_w, top_idx, W1, b1, W2, b2, out):
    F32, F32R, BF16, I32, U32 = (mybir.dt.float32, mybir.dt.float32r, mybir.dt.bfloat16,
                                 mybir.dt.int32, mybir.dt.uint32)
    ALU, ACT = mybir.AluOpType, mybir.ActivationFunctionType
    ds = bass.ds

    P = 128
    NB, S, H = x_in.shape
    N = NB * S
    KH = H // P
    NPAIR = NB // 2
    SCALE = float(H) ** -0.5
    C, NE = top_idx.shape
    FF = W1.shape[2]
    NF = FF // P
    NT = C // P
    ROW = H + NE
    LN_EPS, RMS_EPS = 1e-5, 1e-6
    PIECE = 512
    W1C = KH * FF
    WC = W1C + NF * H
    IDX_PARTS = 4
    NCH = 4
    CH = WC // NCH
    DUP = 1024.0
    SKIP = 4096.0
    MASKED = -1e30

    ctx = ExitStack()
    with ctx:
        def sb(name, shape, dt=F32):
            return ctx.enter_context(nc.sbuf_tensor(name, shape, dt))

        def sem(name):
            return ctx.enter_context(nc.semaphore(name))

        rows_dram = nc.dram_tensor("token_rows", [N, ROW], F32, kind="Internal").ap()

        ident = sb("ident", [P, P])
        causal = sb("causal", [P, 2 * S])
        norm_w_bc = sb("norm_w_bc", [P, 2 * H])
        norm_wT = sb("norm_wT", [P, KH])
        gate_b_bc = sb("gate_b_bc", [P, H])
        Mqk = sb("Mqk", [P, KH, H])
        gateT = sb("gateT", [P, KH, H])
        bias_rows = sb("bias_rows", [NE * NF, P])
        biasT = sb("biasT", [P, NE * NF])
        wts = sb("wts", [P, 3, KH, H])
        x_all = sb("x_all", [P, NB * H])
        idx_all = sb("idx_all", [P, NT, NE], I32)
        idx_f = sb("idx_f", [P, NT * NE])
        idx_rows = sb("idx_rows", [P, C * NE], I32)
        x3 = x_all[:, :].rearrange("p (b h) -> p b h", h=H)

        bn6 = sb("bn6", [P, NB, 6])
        mv = sb("mv", [P, NB, 2])
        pow_in = sb("pow_in", [P, 2, NB])
        pow_out = sb("pow_out", [P, 2, NB])
        half_neg = sb("half_neg", [P, 2, NB])
        rms_t = sb("rms_t", [P, NB])
        rms = sb("rms", [P, NB])

        h = sb("h", [P, 2, 2, H])
        hn_cnat = sb("hn_cnat", [P, 2, 2 * 2 * H])
        normed = sb("normed", [P, 2, 2, H])
        hn = hn_cnat[:, 0, :].rearrange("p (s b h) -> p s b h", s=2, b=2)
        cnat = hn_cnat[:, 1, :].rearrange("p (s b h) -> p s b h", s=2, b=2)
        keysT = sb("keysT", [P, 2, KH, 2 * S])
        hnT = sb("hnT", [P, 2, KH, 2 * S])
        qT = sb("qT", [P, KH, 2 * S])
        probs = sb("probs", [P, 2, 2 * S])
        probsT = sb("probsT", [P, 2, 2, S])
        gate_t = sb("gate_t", [P, 2 * H])
        diff = sb("diff", [P, 2, H])
        x_plus_h = sb("x_plus_h", [P, 2, 2 * H])
        x2 = sb("x2", [P, 2, 2, H])
        xn2 = sb("xn2", [P, 2, 2, H])
        mx = sb("mx", [P, 2])
        neg_mx = sb("neg_mx", [P, 2])
        rsum = sb("rsum", [P, 2])
        rinv = sb("rinv", [P, 2])
        bn6b = sb("bn6b", [P, 2, 6])
        mv2 = sb("mv2", [P, 2, 2, 2])
        var_eps = sb("var_eps", [P, 2, 2])
        rstd2 = sb("rstd2", [P, 2, 2])
        shift2 = sb("shift2", [P, 2, 2])

        w_raw = sb("w_raw", [P, WC])
        w_hi = sb("w_hi", [P, 2, WC], F32R)
        w_lo = sb("w_lo", [P, 2, WC], F32R)
        x_hi = sb("x_hi", [P, 2, KH, C], F32R)
        x_lo = sb("x_lo", [P, 2, KH, C], F32R)
        g_hi = sb("g_hi", [P, 2, C], F32R)
        g_lo = sb("g_lo", [P, 2, C], F32R)
        seen = sb("seen", [P, NT, C], BF16)
        junk = sb("junk", [P, C], BF16)
        total = sb("total", [P, NT])
        factor = sb("factor", [P, NT])
        skip_f = sb("skip_f", [P, NT])
        gidx = sb("gidx", [P, 2, NT], I32)
        sidx = sb("sidx", [P, NT], I32)

        xg = x_all[:, 0:2 * NT * ROW].rearrange("p (s t r) -> p s t r", s=2, t=NT)
        accg = x_all[:, 2 * NT * ROW:2 * NT * ROW + NT * H].rearrange("p (t h) -> p t h", h=H)
        b2_bc = hn_cnat[:, :, :].rearrange("p a c -> p (a c)")
        g32 = keysT[:, :, :, :].rearrange("p f k c -> p f (k c)")
        newrow = h[:, :, :, :].rearrange("p s b h -> p (s b) h")

        banks = [ctx.enter_context(nc.psum_tensor(f"bank{i}", [P, 512], F32)) for i in range(8)]
        ps_hnT = banks[0][:, :].rearrange("p (k b t) -> p k b t", k=KH, b=2)
        ps_cT = banks[1][:, :].rearrange("p (k b t) -> p k b t", k=KH, b=2)
        ps_q = banks[2][:, :].rearrange("p (k t) -> p k t", k=KH)
        ps_log = [banks[3][:, 0:2 * S], banks[4][:, 0:2 * S]]
        ps_gate = banks[5][:, :].rearrange("p (b t) -> p b t", b=2)
        ps_pT = banks[6][:, :].rearrange("p (b j s) -> p b j s", b=2, j=2)
        ps_pv = banks[7][:, :].rearrange("p (b t) -> p b t", b=2)
        ps_up = banks[0:2]
        ps_xT = banks[2:4]
        ps_down = [b[:, 0:H] for b in banks[4:8]]

        x_in_s = [sem(f"x_loaded{g}") for g in range(4)]
        c_in_s = [sem(f"ctx_loaded{s}") for s in range(2)]
        wts_in = sem("qk_weights_loaded")
        gatew_in = sem("gate_weight_loaded")
        bc_in = sem("broadcasts_loaded")
        bias_in = sem("bias_loaded")
        b2_in = sem("b2_loaded")
        idx_in = sem("idx_loaded")
        idxrows_in = sem("idx_rows_loaded")
        comb_in = sem("combine_copied")
        w_in = [sem(f"w_chunk_loaded{c}") for c in range(NCH)]
        consts = sem("pool_constants")
        ident_rdy = sem("ident_ready")
        warm_rdy = sem("warm_up_operand_ready")
        setup_mm = sem("setup_products")
        setup_ev = sem("setup_evacuated")
        idx_rdy = sem("idx_float_ready")
        st_x = sem("x_stats")
        pow_rdy = sem("x_pow_done")
        x_steps = sem("x_stats_steps")
        h_rdy = sem("h_ready")
        hn_rdy = sem("hn_ready")
        n_rdy = sem("normed_ready")
        hnT_mm = sem("hn_transposed")
        cT_mm = sem("context_transposed")
        hnT_ev = sem("hnT_ready")
        nT_ev = sem("normedT_ready")
        cT_ev = sem("contextT_ready")
        q_mm = sem("query_product")
        q_ev = sem("qT_ready")
        log_mm = sem("logits_product")
        log_rdy = sem("masked_logits_max")
        neg_rdy = sem("neg_max_ready")
        exp_rdy = sem("exp_done")
        pT_mm = sem("probs_transposed")
        pT_ev = sem("probsT_ready")
        gate_mm = sem("gate_product")
        gate_rdy = sem("gate_logit_ready")
        tanh_rdy = sem("tanh_done")
        pv_mm = sem("values_product")
        last_steps = sem("last_pair_steps")
        ri_rdy = sem("inverse_sum_ready")
        diff_rdy = sem("diff_ready")
        mix_rdy = sem("mixed_ready")
        xh_rdy = sem("x_plus_h_ready")
        x2_rdy = sem("x2_ready")
        st2 = sem("x2_stats")
        ve_rdy = sem("x2_var_eps_ready")
        rstd_rdy = sem("x2_rstd_ready")
        shift_rdy = sem("x2_shift_ready")
        xn_rdy = sem("xn2_ready")
        x2_out = [sem(f"x2_stored{s}") for s in range(2)]
        xn_out = [sem(f"xn2_stored{s}") for s in range(2)]
        whi_rdy = sem("w_hi_ready")
        wlo_rdy = sem("w_lo_ready")
        gidx_rdy = sem("gather_idx_ready")
        xg_in = [sem(f"rows_gathered{s}") for s in range(2)]
        first_rows_in = [sem(f"first_rows_gathered{t}") for t in range(NT)]
        acc_in = sem("sums_gathered")
        scat = sem("sums_scattered")
        xT_mm = sem("rows_transposed")
        xhi_rdy = sem("x_hi_ready")
        xlo_rdy = sem("x_lo_ready")
        up_mm = sem("up_product")
        g_rdy = sem("gelu_done")
        glo_rdy = sem("g_lo_ready")
        out_mm = sem("expert_output")
        accb_rdy = sem("bias_added_to_sums")
        new_rdy = sem("new_sums_ready")
        tot_rdy = sem("slot_totals")
        skip_rdy = sem("skip_ready")
        fac_rdy = sem("factor_ready")
        sidx_rdy = sem("scatter_idx_ready")

        waits_taken = sem("waits_taken")

        block = ctx.enter_context(nc.Block())

        def take_waits(eng):
            eng.sem_inc(waits_taken, 1)

        def each_item(eng, body):
            body(0, 0, 0)
            with eng.Fori(0, 3) as i:
                body(2 * i + 1, 1, i)
                body(2 * i + 2, 0, i + 1)
            body(7, 1, 3)

        def is_first(item):
            return isinstance(item, int) and item == 0

        def is_last(item):
            return isinstance(item, int) and item == 7

        def w_chunk(e, c):
            if c < KH:
                return W1[ds(e, 1), c * P:(c + 1) * P, :].rearrange("e p f -> p (e f)")
            t = NF // (NCH - KH)
            return W2[ds(e, 1), (c - KH) * t * P:(c - KH + 1) * t * P, :].rearrange("e (f p) d -> p (e f) d", p=P)

        def w_chunk_dst(c):
            dst = w_raw[:, c * CH:(c + 1) * CH]
            return dst if c < KH else dst.rearrange("p (f d) -> p f d", d=H)

        @block.sync
        def _(sp):
            x_v = x_in.rearrange("b s h -> s b h")
            c_v = ctx_in.rearrange("b s h -> s b h")

            def row_broadcast(dst, vec):
                n = vec.shape[0]
                return sp.dma_start(dst, vec.rearrange("(a h) -> a h", a=1).broadcast_to([P, n]))

            def load_x(g, b0, b1_):
                sp.dma_start(x3[:, b0:b1_, :], x_v[:, b0:b1_, :]).then_inc(x_in_s[g], 16)

            def load_ctx(p):
                sp.dma_start(cnat[:, p % 2, :, :], c_v[:, 2 * p:2 * p + 2, :]).then_inc(c_in_s[p % 2], 16)

            def load_weight(n, w, loaded):
                sp.dma_start(wts[:, n, :, :], w.rearrange("(k p) h -> p k h", p=P)).then_inc(loaded, 16)

            load_x(0, 0, 2)
            load_weight(0, q_w, wts_in)
            load_weight(1, k_w, wts_in)
            load_x(1, 2, 4)
            for n in range(2):
                row_broadcast(norm_w_bc[:, n * H:(n + 1) * H], norm_w).then_inc(bc_in, 16)
            sp.dma_start(norm_wT[:, :], norm_w.rearrange("(k p) -> p k", p=P), allow_slow_non_contiguous=True)\
                .then_inc(bc_in, 16)
            load_ctx(0)
            load_weight(2, gate_w, gatew_in)
            row_broadcast(gate_b_bc[:, :], gate_b).then_inc(bc_in, 16)
            load_x(2, 4, 10)
            load_ctx(1)
            load_x(3, 10, NB)
            for c in range(NCH):
                sp.dma_start(w_chunk_dst(c), w_chunk(0, c)).then_inc(w_in[c], 16)
            sp.dma_start(bias_rows[:, :], b1.rearrange("e (f p) -> (e f) p", p=P)).then_inc(bias_in, 16)
            sp.dma_start(idx_all[:, :, :], top_idx.rearrange("(p t) e -> p t e", t=NT)).then_inc(idx_in, 16)
            sp.dma_start(rows_dram[:, H:ROW], comb_w).then_inc(comb_in, 16)
            out_v = out.rearrange("b s h -> s b h")
            rows_v = rows_dram.rearrange("(b s) r -> s b r", s=S)
            for p in range(1, NPAIR + 1):
                if p + 1 < NPAIR:
                    sp.wait_ge(pv_mm, p)
                    load_ctx(p + 1)
                r = p - 1
                sp.wait_ge(x2_rdy, r + 1)
                sp.dma_start(out_v[:, 2 * r:2 * r + 2, :], x2[:, r % 2, :, :]).then_inc(x2_out[r % 2], 16)
                sp.wait_ge(xn_rdy, 2 * r + 2)
                sp.dma_start(rows_v[:, 2 * r:2 * r + 2, 0:H], xn2[:, r % 2, :, :]).then_inc(xn_out[r % 2], 16)
                if p <= IDX_PARTS:
                    n = C * NE // IDX_PARTS
                    row_broadcast(idx_rows[:, r * n:(r + 1) * n], top_idx.rearrange("c e -> (c e)")[r * n:(r + 1) * n])\
                        .then_inc(idxrows_in, 16)
                if r == NPAIR - 1:
                    for t in range(NT):
                        sp.wait_ge(first_rows_in[t], 16)
                if r % 2 == 1:
                    sp.wait_ge(wlo_rdy, r + 1)
                    sp.dma_start(w_chunk_dst(r // 2), w_chunk(1, r // 2)).then_inc(w_in[r // 2], 16)
            sp.wait_ge(pv_mm, NPAIR)
            row_broadcast(b2_bc, b2.rearrange("e h -> (e h)")).then_inc(b2_in, 16)
            with sp.Fori(2, NE) as e:
                for c in range(NCH):
                    sp.wait_ge(wlo_rdy, 8 * e - 8 + 2 * c + 2)
                    sp.dma_start(w_chunk_dst(c), w_chunk(e, c)).then_inc(w_in[c], 16)

        @block.gpsimd
        def _(pool):
            g = nc.gpsimd
            g.memset(junk[:, :], 0.0).then_inc(warm_rdy, 1)
            g.memset(ident[:, :], 0.0).then_inc(consts, 1)
            g.memset(half_neg[:, :, :], -0.5).then_inc(consts, 1)
            g.memset(causal[:, :], 0.0).then_inc(consts, 1)
            g.memset(seen[:, :, :], 1.0).then_inc(consts, 1)
            pool.wait_ge(consts, 4)
            g.affine_select(out=ident[:, :], in_=ident[:, :], compare_op=ALU.not_equal, fill=1.0, base=0,
                            pattern=[[-1, P]], channel_multiplier=1).then_inc(ident_rdy, 1)
            g.affine_select(out=causal[:, 0:S], in_=causal[:, 0:S], compare_op=ALU.is_ge, fill=MASKED, base=0,
                            pattern=[[-1, S]], channel_multiplier=1).then_inc(ident_rdy, 1)

            def x_powers(b0, b1_, n):
                pool.wait_ge(st_x, n)
                g.tensor_tensor(pow_out[:, :, b0:b1_], pow_in[:, :, b0:b1_], half_neg[:, :, b0:b1_], ALU.pow)\
                    .then_inc(pow_rdy, 1)

            def normed_rows(p, s):
                pool.wait_ge(hn_rdy, 2 * p + 2)
                g.tensor_tensor(normed[:, s, :, :].rearrange("p b h -> p (b h)"),
                                hn[:, s, :, :].rearrange("p b h -> p (b h)"), norm_w_bc[:, :], ALU.mult)\
                    .then_inc(n_rdy, 1)

            x_powers(0, 2, 1)
            x_powers(2, 4, 2)
            pool.wait_ge(bc_in, 64)
            normed_rows(0, 0)

            def rstd(r, s):
                pool.wait_ge(ve_rdy, r + 1)
                g.tensor_tensor(rstd2[:, s, :], var_eps[:, s, :], half_neg[:, 0, 0:2], ALU.pow).then_inc(rstd_rdy, 1)

            def attention(p, s, use):
                pool.wait_ge(h_rdy, 2 * p + 2)
                g.tensor_tensor(x_plus_h[:, s, :], x_all[:, ds(p * (2 * H), 2 * H)],
                                h[:, s, :, :].rearrange("p b h -> p (b h)"), ALU.add).then_inc(xh_rdy, 1)
                if not is_last(p):
                    if not is_first(p):
                        pool.wait_ge(pv_mm, p)
                        take_waits(pool)
                    normed_rows(p + 1, 1 - s)
                if is_first(p):
                    x_powers(4, 10, 3)
                    x_powers(10, NB, 4)
                    for t in range(NT):
                        g.affine_select(out=seen[:, t, :], in_=seen[:, t, :], compare_op=ALU.is_ge, fill=DUP, base=-t,
                                        pattern=[[1, C]], channel_multiplier=-NT).then_inc(consts, 1)
                else:
                    rstd(p - 1, 1 - s)

            each_item(pool, attention)
            rstd(7, 1)

            idx = bass.IndirectOffsetOnAxis
            flat = out.rearrange("b s h -> (b s) h")

            def gather_rows(s):
                take_waits(pool)
                for t in range(NT):
                    g.indirect_dma_start(xg[:, s, t, :], None, rows_dram, idx(gidx[:, s, t:t + 1].bitcast(U32), 0))\
                        .then_inc(xg_in[s], 16)

            def gather_sums(s):
                take_waits(pool)
                for t in range(NT):
                    g.indirect_dma_start(accg[:, t, :], None, flat, idx(gidx[:, s, t:t + 1].bitcast(U32), 0))\
                        .then_inc(acc_in, 16)

            def scatter_sums(e):
                for t in range(NT):
                    pool.wait_ge(new_rdy, NT * e + t + 1)
                    take_waits(pool)
                    g.indirect_dma_start(flat, idx(sidx[:, t:t + 1].bitcast(U32), 0), newrow[:, t, :], None,
                                         bounds_check=N - 1, oob_is_err=False).then_inc(scat, 16)

            pool.wait_ge(comb_in, 16)
            for s in range(2):
                pool.wait_ge(xn_out[s], 16 * (NPAIR // 2) + 16)
                pool.wait_ge(x2_out[s], 16 * (NPAIR // 2) + 16)
            pool.wait_ge(gidx_rdy, 1)
            for t in range(NT):
                g.indirect_dma_start(xg[:, 0, t, :], None, rows_dram, idx(gidx[:, 0, t:t + 1].bitcast(U32), 0))\
                    .then_inc(first_rows_in[t], 16)

            def expert(e, s, use):
                if not is_last(e):
                    pool.wait_ge(gidx_rdy, e + 2)
                    gather_rows(1 - s)
                if not is_first(e):
                    scatter_sums(e - 1)
                    pool.wait_ge(scat, 16 * NT * e)
                gather_sums(s)

            each_item(pool, expert)
            scatter_sums(7)
            pool.wait_ge(scat, 16 * NT * NE)

        @block.scalar
        def _(act):
            a = nc.scalar
            for s in range(2):
                act.sem_inc(x2_out[s], 16)
                act.sem_inc(xn_out[s], 16)

            def normed_transposed(p):
                act.wait_ge(hnT_mm, p + 1)
                for k in range(KH):
                    a.activation(keysT[:, :, k, 0:S], ps_hnT[:, k, :, :], ACT.Copy, scale=norm_wT[:, k:k + 1])\
                        .then_inc(nT_ev, 1)

            def hn_transposed(p, s):
                a.copy(hnT[:, s, :, :], ps_hnT.rearrange("p k b t -> p k (b t)")).then_inc(hnT_ev, 1)

            def query(p):
                act.wait_ge(q_mm, p + 1)
                a.copy(qT[:, :, :], ps_q).then_inc(q_ev, 1)

            def context_transposed(p):
                act.wait_ge(cT_mm, p + 1)
                a.copy(keysT[:, :, :, S:2 * S].rearrange("p b k t -> p k b t"), ps_cT).then_inc(cT_ev, 1)

            act.wait_ge(setup_mm, 1)
            a.copy(Mqk[:, 0, :], ps_log[0]).then_inc(setup_ev, 1)
            act.wait_ge(bc_in, 64)
            normed_transposed(0)
            act.wait_ge(setup_mm, 2)
            a.copy(Mqk[:, 1, :], ps_log[1]).then_inc(setup_ev, 1)
            hn_transposed(0, 0)
            query(0)
            context_transposed(0)
            act.wait_ge(setup_mm, 3)
            a.copy(gateT[:, :, :], ps_gate).then_inc(setup_ev, 1)

            def normalised_x2(r, s, use):
                act.wait_ge(xn_out[s], 16 * use + 16)
                act.wait_ge(shift_rdy, r + 1)
                for b in range(2):
                    a.activation(xn2[:, s, b, :], x2[:, s, b, :], ACT.Identity, bias=shift2[:, s, b:b + 1],
                                 scale=rstd2[:, s, b:b + 1]).then_inc(xn_rdy, 1)

            def expert0_hi(p):
                col = ds(p * PIECE, PIECE)
                a.copy(w_hi[:, 0, col], w_raw[:, col]).then_inc(whi_rdy, 1)

            def attention(p, s, use):
                for b in range(2):
                    act.wait_ge(neg_rdy, 2 * p + b + 1)
                    a.activation(probs[:, b, :], probs[:, b, :], ACT.Exp, bias=neg_mx[:, b:b + 1], scale=SCALE,
                                 accum_out=rsum[:, b:b + 1]).then_inc(exp_rdy, 1)
                if not is_last(p):
                    normed_transposed(p + 1)
                    hn_transposed(p + 1, 1 - s)
                act.wait_ge(pT_mm, p + 1)
                a.copy(probsT[:, :, :, :], ps_pT).then_inc(pT_ev, 1)
                if is_first(p):
                    for c in range(NCH):
                        act.wait_ge(w_in[c], 16)
                if not is_last(p):
                    expert0_hi(p)
                act.wait_ge(gate_rdy, 2 * p + 2)
                a.activation(gate_t[:, :], gate_t[:, :], ACT.Tanh, scale=0.5).then_inc(tanh_rdy, 1)
                if not is_last(p):
                    query(p + 1)
                    context_transposed(p + 1)
                if not is_first(p):
                    normalised_x2(p - 1, 1 - s, use if s == 1 else use - 1)

            each_item(act, attention)
            normalised_x2(7, 1, 3)
            expert0_hi(NPAIR - 1)
            act.wait_ge(setup_mm, 4)
            a.copy(biasT[:, :], banks[0][:, 0:NE * NF]).then_inc(setup_ev, 1)

            def x_hi_part(e, s):
                for k in range(KH):
                    act.wait_ge(xT_mm, KH * e + k + 1)
                    a.copy(x_hi[:, s, k, :], ps_xT[k][:, :]).then_inc(xhi_rdy, 1)

            x_hi_part(0, 0)

            def expert(e, s, use):
                for f in range(NF):
                    act.wait_ge(up_mm, NF * e + f + 1)
                    bias = biasT[:, ds(e * NF + f, 1)]
                    a.activation(g32[:, f % 2, :], ps_up[f % 2][:, :], ACT.Gelu_apprx_tanh, bias=bias)
                    a.activation(g_hi[:, f % 2, :], ps_up[f % 2][:, :], ACT.Gelu_apprx_tanh, bias=bias)\
                        .then_inc(g_rdy, 1)
                    if not is_last(e):
                        if f % 2 == 0:
                            act.wait_ge(w_in[f // 2], 16 * e + 32)
                        col = slice(f * PIECE, (f + 1) * PIECE)
                        a.copy(w_hi[:, 1 - s, col], w_raw[:, col]).then_inc(whi_rdy, 1)
                        if f == 4:
                            x_hi_part(e + 1, 1 - s)

            each_item(act, expert)

        @block.vector
        def _(dve):
            v = nc.vector

            steps = [0]

            def x_stats(b0, b1_, group):
                dve.wait_ge(x_in_s[group], 16)
                for b in range(b0, b1_):
                    v.bn_stats(bn6[:, b, :], x3[:, b, :]).then_inc(x_steps, 1)
                steps[0] += b1_ - b0
                dve.wait_ge(x_steps, steps[0])
                for b in range(b0, b1_):
                    v.bn_aggr(mv[:, b, :], bn6[:, b, :]).then_inc(x_steps, 1)
                steps[0] += b1_ - b0

            def x_variances(b0, b1_):
                dve.wait_ge(x_steps, steps[0])
                v.tensor_scalar(pow_in[:, 0, b0:b1_], mv[:, b0:b1_, 1], LN_EPS, None, ALU.add)
                v.tensor_scalar(pow_in[:, 1, b0:b1_], mv[:, b0:b1_, 1], 1.0 + RMS_EPS, LN_EPS * RMS_EPS,
                                ALU.mult, ALU.add).then_inc(st_x, 1)

            def x_rms(b0, b1_, n):
                dve.wait_ge(pow_rdy, n)
                v.tensor_tensor(rms_t[:, b0:b1_], pow_in[:, 1, b0:b1_], pow_out[:, 1, b0:b1_], ALU.mult)\
                    .then_inc(x_steps, 1)
                steps[0] += 1
                dve.wait_ge(x_steps, steps[0])
                v.tensor_tensor(rms[:, b0:b1_], rms_t[:, b0:b1_], pow_out[:, 0, b0:b1_], ALU.mult)\
                    .then_inc(x_steps, 1)
                steps[0] += 1

            mvf = mv[:, :, :].rearrange("p b c -> p (b c)")

            def hn_rows(p, s):
                for b in range(2):
                    v.tensor_scalar(hn[:, s, b, :], x_all[:, ds((2 * p + b) * H, H)], mvf[:, ds(4 * p + 2 * b, 1)],
                                    pow_out[:, 1, ds(2 * p + b, 1)], ALU.subtract, ALU.mult).then_inc(hn_rdy, 1)

            def h_rows(p, s, reused=True):
                if reused:
                    dve.wait_ge(xh_rdy, p - 1)
                    dve.wait_ge(diff_rdy, 2 * p - 2)
                for b in range(2):
                    v.tensor_scalar(h[:, s, b, :], x_all[:, ds((2 * p + b) * H, H)], mvf[:, ds(4 * p + 2 * b, 1)],
                                    pow_out[:, 0, ds(2 * p + b, 1)], ALU.subtract, ALU.mult).then_inc(h_rdy, 1)

            x_stats(0, 2, 0)
            x_variances(0, 2)
            dve.wait_ge(pow_rdy, 1)
            hn_rows(0, 0)
            x_stats(2, 4, 1)
            x_variances(2, 4)
            h_rows(0, 0, False)
            dve.wait_ge(pow_rdy, 2)
            hn_rows(1, 1)
            h_rows(1, 1, False)
            x_rms(0, 4, 2)
            x_stats(4, 10, 2)
            x_variances(4, 10)
            dve.wait_ge(ident_rdy, 2)
            dve.wait_ge(bc_in, 64)

            def finish_diff(p, s):
                for b in range(2):
                    if b == 0:
                        dve.wait_ge(pv_mm, p + 1)
                        dve.wait_ge(ri_rdy, p + 1)
                    v.scalar_tensor_tensor(diff[:, b, :], ps_pv[:, b, :], rinv[:, b:b + 1], h[:, s, b, :],
                                           ALU.mult, ALU.subtract).then_inc(diff_rdy, 1)

            def mix(p):
                dve.wait_ge(tanh_rdy, p + 1)
                dve.wait_ge(diff_rdy, 2 * p + 2)
                d = diff[:, :, :].rearrange("p b h -> p (b h)")
                v.scalar_tensor_tensor(d, gate_t[:, :], 1.0, d, ALU.add, ALU.mult).then_inc(mix_rdy, 1)

            def residual(p, s, use):
                dve.wait_ge(mix_rdy, p + 1)
                dve.wait_ge(xh_rdy, p + 1)
                dve.wait_ge(x2_out[s], 16 * use + 16)
                v.scalar_tensor_tensor(x2[:, s, :, :].rearrange("p b h -> p (b h)"),
                                       diff[:, :, :].rearrange("p b h -> p (b h)"), 0.5, x_plus_h[:, s, :],
                                       ALU.mult, ALU.add).then_inc(x2_rdy, 1)

            def stats2(p, s):
                dve.wait_ge(x2_rdy, p + 1)
                for b in range(2):
                    v.bn_stats(bn6b[:, b, :], x2[:, s, b, :]).then_inc(st2, 1)

            def aggr2(p, s):
                for b in range(2):
                    dve.wait_ge(st2, 4 * p + b + 1)
                    take_waits(dve)
                    v.bn_aggr(mv2[:, s, b, :], bn6b[:, b, :]).then_inc(st2, 1)
                dve.wait_ge(st2, 4 * p + 4)
                v.tensor_scalar(var_eps[:, s, :], mv2[:, s, :, 1], LN_EPS, None, ALU.add).then_inc(ve_rdy, 1)

            def shift(r, s):
                dve.wait_ge(rstd_rdy, r + 1)
                v.scalar_tensor_tensor(shift2[:, s, :], mv2[:, s, :, 0], -1.0, rstd2[:, s, :], ALU.mult, ALU.mult)\
                    .then_inc(shift_rdy, 1)

            def expert0_lo(p):
                dve.wait_ge(whi_rdy, p + 1)
                col = ds(p * PIECE, PIECE)
                v.tensor_tensor(w_lo[:, 0, col], w_raw[:, col], w_hi[:, 0, col].bitcast(F32), ALU.subtract)\
                    .then_inc(wlo_rdy, 1)

            def attention(p, s, use):
                last_use = use if s == 1 else use - 1
                if not is_first(p):
                    if not is_last(p):
                        dve.wait_ge(n_rdy, p)
                        hn_rows(p + 1, 1 - s)
                    finish_diff(p - 1, 1 - s)
                    dve.wait_ge(pT_mm, p)
                for b in range(2):
                    dve.wait_ge(log_mm, 2 * p + b + 1)
                    take_waits(dve)
                    v.tensor_tensor_reduce(out=probs[:, b, :], in0=ps_log[b], in1=causal[:, :], scale=1.0,
                                           scalar=-3.0e38, op0=ALU.add, op1=ALU.max, accum_out=mx[:, b:b + 1])\
                        .then_inc(log_rdy, 1)
                for b in range(2):
                    dve.wait_ge(log_rdy, 2 * p + b + 1)
                    v.tensor_scalar(neg_mx[:, b:b + 1], mx[:, b:b + 1], -SCALE, None, ALU.mult).then_inc(neg_rdy, 1)
                if not is_first(p):
                    mix(p - 1)
                    residual(p - 1, 1 - s, last_use)
                    stats2(p - 1, 1 - s)
                else:
                    x_stats(10, NB, 3)
                dve.wait_ge(gate_mm, p + 1)
                if is_first(p):
                    dve.wait_ge(x_steps, steps[0])
                else:
                    dve.wait_ge(mix_rdy, p)
                for b in range(2):
                    v.scalar_tensor_tensor(gate_t[:, b * H:(b + 1) * H], ps_gate[:, b, :], rms[:, ds(2 * p + b, 1)],
                                           gate_b_bc[:, :], ALU.mult, ALU.add).then_inc(gate_rdy, 1)
                if is_first(p):
                    x_variances(10, NB)
                else:
                    aggr2(p - 1, 1 - s)
                    if not is_last(p):
                        h_rows(p + 1, 1 - s)
                dve.wait_ge(exp_rdy, 2 * p + 2)
                v.reciprocal(rinv[:, :], rsum[:, :]).then_inc(ri_rdy, 1)
                if not is_last(p):
                    expert0_lo(p)
                if is_first(p):
                    x_rms(4, NB, 4)
                    dve.wait_ge(x_steps, steps[0])
                elif not is_last(p):
                    shift(p - 1, 1 - s)

            each_item(dve, attention)
            dve.wait_ge(idx_in, 16)
            v.tensor_copy(idx_f[:, :], idx_all[:, :, :].rearrange("p t e -> p (t e)")).then_inc(idx_rdy, 1)
            v.tensor_copy(gidx[:, 0, :], idx_all[:, :, 0]).then_inc(gidx_rdy, 1)

            last_s = (NPAIR - 1) % 2

            def last_pair_diff(b):
                v.scalar_tensor_tensor(diff[:, b, :], ps_pv[:, b, :], rinv[:, b:b + 1], h[:, last_s, b, :],
                                       ALU.mult, ALU.subtract).then_inc(last_steps, 1)

            dve.wait_ge(mix_rdy, NPAIR - 1)
            dve.wait_ge(ri_rdy, NPAIR)
            dve.wait_ge(pv_mm, NPAIR)
            last_pair_diff(0)
            last_pair_diff(1)
            shift(NPAIR - 2, 1 - last_s)
            dve.wait_ge(tanh_rdy, NPAIR)
            for b in range(2):
                dve.wait_ge(last_steps, b + 1)
                v.scalar_tensor_tensor(diff[:, b, :], gate_t[:, b * H:(b + 1) * H], 1.0, diff[:, b, :],
                                       ALU.add, ALU.mult).then_inc(last_steps, 1)
            dve.wait_ge(xh_rdy, NPAIR)
            dve.wait_ge(x2_out[last_s], 16 * (NPAIR // 2))
            for b in range(2):
                dve.wait_ge(last_steps, b + 3)
                x2_half = v.scalar_tensor_tensor(x2[:, last_s, b, :], diff[:, b, :], 0.5,
                                                 x_plus_h[:, last_s, b * H:(b + 1) * H], ALU.mult, ALU.add)
                x2_half.then_inc(last_steps if b == 0 else x2_rdy, 1)
            for b in range(2):
                if b == 0:
                    dve.wait_ge(last_steps, 5)
                else:
                    dve.wait_ge(x2_rdy, NPAIR)
                v.bn_stats(bn6b[:, b, :], x2[:, last_s, b, :]).then_inc(st2, 1)
            aggr2(NPAIR - 1, last_s)
            shift(NPAIR - 1, last_s)
            expert0_lo(NPAIR - 1)

            def x_lo_part(e, s):
                for k in range(KH):
                    dve.wait_ge(xhi_rdy, KH * e + k + 1)
                    v.tensor_tensor(x_lo[:, s, k, :], ps_xT[k][:, :], x_hi[:, s, k, :].bitcast(F32), ALU.subtract)\
                        .then_inc(xlo_rdy, 1)

            def add_bias(e, tiles):
                dve.wait_ge(acc_in, 16 * NT * (e + 1))
                dve.wait_ge(fac_rdy, e + 1)
                for t in tiles:
                    v.scalar_tensor_tensor(accg[:, t, :], b2_bc[:, ds(e * H, H)], factor[:, t:t + 1], accg[:, t, :],
                                           ALU.mult, ALU.add).then_inc(accb_rdy, 1)

            def new_sums(e):
                dve.wait_ge(accb_rdy, NT * e + NT)
                for t in range(NT):
                    dve.wait_ge(out_mm, NT * e + t + 1)
                    v.scalar_tensor_tensor(newrow[:, t, :], ps_down[t], factor[:, t:t + 1],
                                           accg[:, t, :], ALU.mult, ALU.add).then_inc(new_rdy, 1)

            TOTALS_AT = (1, 2, 3, 4)
            rows_by_expert = idx_rows[:, :].rearrange("p (c e) -> p e c", e=NE)

            def slot_total(e, t):
                v.scalar_tensor_tensor(junk[:, :], rows_by_expert[:, ds(e, 1), :].rearrange("p a c -> p (a c)"),
                                       idx_f[:, ds(t * NE + e, 1)], seen[:, t, :], ALU.is_equal, ALU.mult,
                                       accum_out=total[:, t:t + 1]).then_inc(tot_rdy, 1)

            x_lo_part(0, 0)

            def expert(e, s, use):
                if not is_last(e):
                    if not is_first(e):
                        dve.wait_ge(acc_in, 16 * NT * e)
                    v.tensor_copy(gidx[:, 1 - s, :], idx_all[:, :, ds(e + 1, 1)].rearrange("p t a -> p (t a)"))\
                        .then_inc(gidx_rdy, 1)
                for f in range(NF):
                    dve.wait_ge(g_rdy, NF * e + f + 1)
                    v.tensor_tensor(g_lo[:, f % 2, :], g32[:, f % 2, :], g_hi[:, f % 2, :].bitcast(F32), ALU.subtract)\
                        .then_inc(glo_rdy, 1)
                    if f == 0 and not is_first(e):
                        new_sums(e - 1)
                    if not is_last(e):
                        col = slice(f * PIECE, (f + 1) * PIECE)
                        dve.wait_ge(whi_rdy, 8 * e + 8 + f + 1)
                        v.tensor_tensor(w_lo[:, 1 - s, col], w_raw[:, col], w_hi[:, 1 - s, col].bitcast(F32),
                                        ALU.subtract).then_inc(wlo_rdy, 1)
                        if f == 5:
                            x_lo_part(e + 1, 1 - s)
                    if f in TOTALS_AT:
                        n = TOTALS_AT.index(f)
                        if is_first(e) and n == 0:
                            dve.wait_ge(idxrows_in, 16 * IDX_PARTS)
                            dve.wait_ge(idx_rdy, 1)
                            dve.wait_ge(consts, 4 + NT)
                        if not is_first(e):
                            dve.wait_ge(tot_rdy, NT * e + n)
                        elif n:
                            dve.wait_ge(tot_rdy, n)
                        slot_total(e, n)
                    if f == 6:
                        dve.wait_ge(tot_rdy, NT * e + NT)
                        v.tensor_tensor(factor[:, :], total[:, :],
                                        xg[:, s, :, ds(e + H, 1)].rearrange("p t a -> p (t a)"), ALU.mult)\
                            .then_inc(fac_rdy, 1)
                        v.tensor_scalar(skip_f[:, :], total[:, :], DUP, SKIP, ALU.is_ge, ALU.mult).then_inc(skip_rdy, 1)
                        dve.wait_ge(skip_rdy, e + 1)
                        if not is_first(e):
                            dve.wait_ge(scat, 16 * NT * e)
                        v.tensor_tensor(sidx[:, :], skip_f[:, :],
                                        idx_f[:, :].rearrange("p (t e) -> p t e", e=NE)[:, :, ds(e, 1)]
                                        .rearrange("p t a -> p (t a)"), ALU.add).then_inc(sidx_rdy, 1)
                        if is_first(e):
                            dve.wait_ge(b2_in, 16)
                        add_bias(e, range(NT) if is_last(e) else range(NT // 2))
                    if f == NF - 1 and not is_last(e):
                        add_bias(e, range(NT // 2, NT))

            each_item(dve, expert)
            dve.wait_ge(sidx_rdy, NE)
            new_sums(7)

        @block.tensor
        def _(pe):
            t_ = nc.tensor

            def keep_warm(n):
                for _ in range(n):
                    t_.matmul(banks[7][:, :], junk[:, 0:P], junk[:, :], start=True, stop=True)

            pe.wait_ge(warm_rdy, 1)
            keep_warm(10)
            pe.wait_ge(wts_in, 32)
            pe.wait_ge(ident_rdy, 2)
            def M_rows(m):
                for k in range(KH):
                    last = t_.matmul(ps_log[m], wts[:, 0, k, m * P:(m + 1) * P], wts[:, 1, k, :],
                                     start=(k == 0), stop=(k == KH - 1))
                last.then_inc(setup_mm, 1)

            def hn_transposes(p, s):
                pe.wait_ge(hn_rdy, 2 * p + 2)
                if not is_first(p):
                    pe.wait_ge(hnT_ev, p)
                for k in range(KH):
                    for b in range(2):
                        last = t_.transpose(ps_hnT[:, k, b, :], hn[:, s, b, k * P:(k + 1) * P], ident[:, :])
                last.then_inc(hnT_mm, 1)

            def context_transposes(p, s, use):
                pe.wait_ge(c_in_s[s], 16 * use + 16)
                for k in range(KH):
                    for b in range(2):
                        last = t_.transpose(ps_cT[:, k, b, :], cnat[:, s, b, k * P:(k + 1) * P], ident[:, :])
                last.then_inc(cT_mm, 1)

            def query(p):
                pe.wait_ge(nT_ev, 2 * p + 2)
                for m in range(KH):
                    for k in range(KH):
                        last = t_.matmul(ps_q[:, m, :].rearrange("p (b t) -> p b t", b=2), Mqk[:, k, m * P:(m + 1) * P],
                                         keysT[:, :, k, 0:S], start=(k == 0), stop=(k == KH - 1))
                last.then_inc(q_mm, 1)

            M_rows(0)
            hn_transposes(0, 0)
            M_rows(1)
            pe.wait_ge(setup_ev, 2)
            query(0)
            context_transposes(0, 0, 0)
            pe.wait_ge(gatew_in, 16)
            for k in range(KH):
                for o in range(KH):
                    last = t_.transpose(ps_gate[:, k, o * P:(o + 1) * P], wts[:, 2, o, k * P:(k + 1) * P], ident[:, :])
            last.then_inc(setup_mm, 1)

            def attention(p, s, use):
                pe.wait_ge(q_ev, p + 1)
                pe.wait_ge(cT_ev, p + 1)
                for b in range(2):
                    if not is_first(p):
                        pe.wait_ge(log_rdy, 2 * p - 1 + b)
                    for k in range(KH):
                        last = t_.matmul(ps_log[b], qT[:, k, b * S:(b + 1) * S], keysT[:, b, k, :],
                                         start=(k == 0), stop=(k == KH - 1))
                    last.then_inc(log_mm, 1)
                if not is_last(p):
                    hn_transposes(p + 1, 1 - s)
                pe.wait_ge(hnT_ev, p + 1)
                if is_first(p):
                    pe.wait_ge(setup_ev, 3)
                else:
                    pe.wait_ge(gate_rdy, 2 * p)
                for b in range(2):
                    for k in range(KH):
                        last = t_.matmul(ps_gate[:, b, :], hnT[:, s, k, b * S:(b + 1) * S], gateT[:, k, :],
                                         start=(k == 0), stop=(k == KH - 1))
                last.then_inc(gate_mm, 1)
                pe.wait_ge(exp_rdy, 2 * p + 2)
                for b in range(2):
                    for j in range(2):
                        last = t_.transpose(ps_pT[:, b, j, :], probs[:, b, j * S:(j + 1) * S], ident[:, :])
                last.then_inc(pT_mm, 1)
                if not is_last(p):
                    query(p + 1)
                    context_transposes(p + 1, 1 - s, use if s == 0 else use + 1)
                pe.wait_ge(pT_ev, p + 1)
                pe.wait_ge(n_rdy, p + 1)
                if not is_first(p):
                    pe.wait_ge(diff_rdy, 2 * p)
                for b in range(2):
                    for j in range(2):
                        values = normed if j == 0 else cnat
                        last = t_.matmul(ps_pv[:, b, :], probsT[:, b, j, :], values[:, s, b, :],
                                         start=(j == 0), stop=(j == 1))
                last.then_inc(pv_mm, 1)

            each_item(pe, attention)
            pe.wait_ge(bias_in, 16)
            t_.transpose(banks[0][:, 0:NE * NF], bias_rows[:, :], ident[0:NE * NF, 0:NE * NF]).then_inc(setup_mm, 1)

            def three_passes(dst, lhs_hi, lhs_lo, rhs_hi, rhs_lo, first, last_one):
                t_.matmul(dst, lhs_hi, rhs_hi, start=first, stop=False)
                t_.matmul(dst, lhs_hi, rhs_lo, start=False, stop=False)
                return t_.matmul(dst, lhs_lo, rhs_hi, start=False, stop=last_one)

            def rows_transposed(e, s, rounds):
                pe.wait_ge(xg_in[s], 16 * NT * rounds)
                pe.wait_ge(xlo_rdy, KH * e)
                for k in range(KH):
                    for t in range(NT):
                        last = t_.transpose(ps_xT[k][:, t * P:(t + 1) * P], xg[:, s, t, k * P:(k + 1) * P], ident[:, :])
                    last.then_inc(xT_mm, 1)

            def up(e, s, f):
                if not (is_first(e) and f < 2):
                    pe.wait_ge(g_rdy, NF * e + f - 1)
                if f == 0:
                    pe.wait_ge(wlo_rdy, 8 * e + 4)
                    dst = ps_up[0][:, :]
                    for k in range(KH):
                        c = slice(k * FF, k * FF + P)
                        pe.wait_ge(xhi_rdy, KH * e + k + 1)
                        t_.matmul(dst, w_hi[:, s, c], x_hi[:, s, k, :], start=(k == 0), stop=False)
                        t_.matmul(dst, w_lo[:, s, c], x_hi[:, s, k, :], start=False, stop=False)
                    for k in range(KH):
                        pe.wait_ge(xlo_rdy, KH * e + k + 1)
                        last = t_.matmul(dst, w_hi[:, s, k * FF:k * FF + P], x_lo[:, s, k, :], start=False,
                                         stop=(k == KH - 1))
                    last.then_inc(up_mm, 1)
                    return
                for k in range(KH):
                    c = slice(k * FF + f * P, k * FF + (f + 1) * P)
                    last = three_passes(ps_up[f % 2][:, :], w_hi[:, s, c], w_lo[:, s, c], x_hi[:, s, k, :],
                                        x_lo[:, s, k, :], k == 0, k == KH - 1)
                last.then_inc(up_mm, 1)

            def down(e, s, f):
                if f == 0:
                    pe.wait_ge(wlo_rdy, 8 * e + 8)
                pe.wait_ge(glo_rdy, NF * e + f + 1)
                for t in range(NT):
                    if f == 0 and not is_first(e):
                        pe.wait_ge(new_rdy, NT * e - NT + t + 1)
                    g = slice(t * P, (t + 1) * P)
                    c = slice(W1C + f * H, W1C + (f + 1) * H)
                    last = three_passes(ps_down[t], g_hi[:, f % 2, g], g_lo[:, f % 2, g], w_hi[:, s, c],
                                        w_lo[:, s, c], f == 0, f == NF - 1)
                    if f == NF - 1:
                        last.then_inc(out_mm, 1)

            for s in range(2):
                pe.wait_ge(xn_out[s], 16 * (NPAIR // 2) + 16)
            keep_warm(8)
            for t in range(NT):
                pe.wait_ge(first_rows_in[t], 16)
                for k in range(KH):
                    last = t_.transpose(ps_xT[k][:, t * P:(t + 1) * P], xg[:, 0, t, k * P:(k + 1) * P], ident[:, :])
                    if t == NT - 1:
                        last.then_inc(xT_mm, 1)
                if t < NT - 1:
                    keep_warm(2)

            def expert(e, s, use):
                up(e, s, 0)
                if not is_first(e):
                    down(e - 1, 1 - s, NF - 1)
                up(e, s, 1)
                down(e, s, 0)
                for f in range(2, NF):
                    if f == 4 and not is_last(e):
                        rows_transposed(e + 1, 1 - s, use + 1)
                    up(e, s, f)
                    down(e, s, f - 1)

            each_item(pe, expert)
            down(7, 1, NF - 1)


_INS = ['x', 'ctx_1024', 'L0_xattn_q_w', 'L0_xattn_k_w', 'L0_xattn_norm_w', 'L0_xattn_gate_w', 'L0_xattn_gate_b',
        'L0_ffn_combine_weights', 'L0_ffn_top_idx', 'L0_ffn_W1', 'L0_ffn_b1', 'L0_ffn_W2', 'L0_ffn_b2']


def kernel(**inputs):
    import numpy as _np
    import concourse.bacc as _bacc
    from concourse import mybir as _mybir
    from concourse.bass_utils import run_bass_kernel_spmd as _run

    nc = _bacc.Bacc("TRN2", target_bir_lowering=False, num_devices=1)
    arrays, args = {}, []
    for name in _INS:
        a = _np.ascontiguousarray(inputs[name])
        arrays[f"in_{name}_dram"] = a
        args.append(nc.dram_tensor(f"in_{name}_dram", a.shape, _mybir.dt.from_np(a.dtype), kind="ExternalInput").ap())
    args.append(nc.dram_tensor("out_0_dram", inputs["x"].shape, _mybir.dt.float32, kind="ExternalOutput").ap())
    build_xattn_moe(nc, *args)
    r = _run(nc, [arrays], core_ids=[0])
    return r.results[0]["out_0_dram"]
```

```python
import concourse.bass as bass
from concourse import mybir
from contextlib import ExitStack


def build_xattn_moe(nc, x_in, ctx_in, q_w, k_w, norm_w, gate_w, gate_b, comb_w, top_idx, W1, b1, W2, b2, out):
    F32, F32R, BF16, I32, U32 = (mybir.dt.float32, mybir.dt.float32r, mybir.dt.bfloat16,
                                 mybir.dt.int32, mybir.dt.uint32)
    ALU, ACT = mybir.AluOpType, mybir.ActivationFunctionType
    ds = bass.ds

    P = 128
    NB, S, H = x_in.shape
    N = NB * S
    KH = H // P
    NPAIR = NB // 2
    SCALE = float(H) ** -0.5
    C, NE = top_idx.shape
    FF = W1.shape[2]
    NF = FF // P
    NT = C // P
    ROW = H + NE
    LN_EPS, RMS_EPS = 1e-5, 1e-6
    PIECE = 512
    W1C = KH * FF
    WC = W1C + NF * H
    X_GROUPS = ((0, 2), (2, 4), (4, 10), (10, NB))
    IDX_PARTS = 8
    NCH = 4
    CH = WC // NCH
    DUP = 1024.0
    SKIP = 4096.0
    MASKED = -1e30
    LAST = 7
    assert NPAIR == LAST + 1 and NE == LAST + 1

    ctx = ExitStack()
    with ctx:
        def sb(name, shape, dt=F32):
            return ctx.enter_context(nc.sbuf_tensor(name, shape, dt))

        def sem(name):
            return ctx.enter_context(nc.semaphore(name))

        rows_dram = nc.dram_tensor("token_rows", [N, ROW], F32, kind="Internal").ap()

        ident = sb("ident", [P, P])
        causal = sb("causal", [P, 2 * S])
        norm_w_bc = sb("norm_w_bc", [P, 2 * H])
        norm_wT = sb("norm_wT", [P, KH])
        gate_b_bc = sb("gate_b_bc", [P, H])
        M_hi = sb("M_hi", [P, KH, H], F32R)
        M_lo = sb("M_lo", [P, KH, H], F32R)
        gateT_hi = sb("gateT_hi", [P, KH, H], F32R)
        gateT_lo = sb("gateT_lo", [P, KH, H], F32R)
        bias_rows = sb("bias_rows", [NE * NF, P])
        biasT = sb("biasT", [P, NE * NF])
        setup_or_probs = sb("setup_or_probs", [P, 3, KH * H])
        wts = setup_or_probs[:, :, :].rearrange("p n (k h) -> p n k h", k=KH)
        gate_t = setup_or_probs[:, 0, :]
        probs = setup_or_probs[:, 1, :].rearrange("p (b c) -> p b c", b=2)
        probsT = setup_or_probs[:, 2, :].rearrange("p (b j c) -> p b j c", b=2, j=2)
        x_all = sb("x_all", [P, NB * H])
        idx_all = sb("idx_all", [P, NT, NE], I32)
        idx_f = sb("idx_f", [P, NT * NE])
        idx_rows = sb("idx_rows", [P, C * NE], I32)
        x3 = x_all[:, :].rearrange("p (b h) -> p b h", h=H)

        bn6 = sb("bn6", [P, NB, 6])
        mv = sb("mv", [P, NB, 2])
        pow_in = sb("pow_in", [P, 2, NB])
        pow_out = sb("pow_out", [P, 2, NB])
        half_neg = sb("half_neg", [P, 2, NB])
        rms_t = sb("rms_t", [P, NB])
        rms = sb("rms", [P, NB])

        h = sb("h", [P, 2, 2, H])
        hn_cnat = sb("hn_cnat", [P, 2, 2 * 2 * H])
        normed = sb("normed", [P, 2, 2, H])
        hn = hn_cnat[:, 0, :].rearrange("p (s b h) -> p s b h", s=2, b=2)
        cnat = hn_cnat[:, 1, :].rearrange("p (s b h) -> p s b h", s=2, b=2)
        keysT = sb("keysT", [P, 2, 2, KH, 2 * S])
        hnT_hi = sb("hnT_hi", [P, 2, KH, 2 * S], F32R)
        hnT_lo = sb("hnT_lo", [P, 2, KH, 2 * S], F32R)
        qT = sb("qT", [P, KH, 2 * S])
        diff = sb("diff", [P, 2, H])
        x_plus_h = sb("x_plus_h", [P, 2, 2 * H])
        x2 = sb("x2", [P, 2, 2, H])
        xn2 = sb("xn2", [P, 2, 2, H])
        mx = sb("mx", [P, 2])
        neg_mx = sb("neg_mx", [P, 2])
        rsum = sb("rsum", [P, 2])
        rinv = sb("rinv", [P, 2])
        bn6b = sb("bn6b", [P, 2, 6])
        mv2 = sb("mv2", [P, 2, 2, 2])
        var_eps = sb("var_eps", [P, 2, 2])
        rstd2 = sb("rstd2", [P, 2, 2])
        shift2 = sb("shift2", [P, 2, 2])

        w_raw = sb("w_raw", [P, WC])
        w_hi = sb("w_hi", [P, 2, WC], F32R)
        w_lo = sb("w_lo", [P, 2, WC], F32R)
        x_hi = sb("x_hi", [P, 2, KH, C], F32R)
        x_lo = sb("x_lo", [P, 2, KH, C], F32R)
        g_hi = sb("g_hi", [P, 2, C], F32R)
        g_lo = sb("g_lo", [P, 2, C], F32R)
        junk = sb("junk", [P, C], BF16)
        total = sb("total", [P, NT])
        factor = sb("factor", [P, NT])
        skip_f = sb("skip_f", [P, NT])
        gidx = sb("gidx", [P, 2, NT], I32)
        sidx = sb("sidx", [P, NT], I32)

        xg = x_all[:, 0:2 * NT * ROW].rearrange("p (s t r) -> p s t r", s=2, t=NT)
        accg = x_all[:, 2 * NT * ROW:2 * NT * ROW + NT * H].rearrange("p (t h) -> p t h", h=H)
        seen = normed[:, :, :, :].rearrange("p s b h -> p (s b h)").bitcast(BF16)\
            .rearrange("p (t c) -> p t c", t=NT)
        b2_bc = hn_cnat[:, :, :].rearrange("p a c -> p (a c)")
        g32 = keysT[:, 0, :, :, :].rearrange("p f k c -> p f (k c)")
        newrow = h[:, :, :, :].rearrange("p s b h -> p (s b) h")

        banks = [ctx.enter_context(nc.psum_tensor(f"bank{i}", [P, 512], F32)) for i in range(8)]
        ps_hnT = banks[0][:, :].rearrange("p (k b t) -> p k b t", k=KH, b=2)
        ps_cT = banks[1][:, :].rearrange("p (k b t) -> p k b t", k=KH, b=2)
        ps_q = banks[2][:, :].rearrange("p (k t) -> p k t", k=KH)
        ps_log = [banks[3][:, 0:2 * S], banks[4][:, 0:2 * S]]
        ps_gate = banks[5][:, :].rearrange("p (b t) -> p b t", b=2)
        ps_pT = banks[6][:, :].rearrange("p (b j s) -> p b j s", b=2, j=2)
        ps_pv = banks[7][:, :].rearrange("p (b t) -> p b t", b=2)
        ps_up = banks[0:2]
        ps_xT = banks[2:4]
        ps_down = [b[:, 0:H] for b in banks[4:8]]
        ps_xT0 = [[banks[2 + 4 * half + k][:, 0:C // 2] for k in range(KH)] for half in range(2)]

        x_in_s = [sem(f"x_loaded{g}") for g in range(4)]
        c_in_s = [sem(f"ctx_loaded{s}") for s in range(2)]
        wts_in = sem("qk_weights_loaded")
        gatew_in = sem("gate_weight_loaded")
        bc_in = sem("broadcasts_loaded")
        nwT_in = sem("norm_w_by_partition_loaded")
        bias_in = sem("bias_loaded")
        b2_in = sem("b2_loaded")
        idx_in = sem("idx_loaded")
        idxrows_in = sem("idx_rows_loaded")
        comb_in = sem("combine_copied")
        w_in = [sem(f"w_chunk_loaded{c}") for c in range(NCH)]
        consts = sem("pool_constants")
        ident_rdy = sem("ident_ready")
        seen_rdy = sem("seen_weights_ready")
        warm_rdy = sem("warm_up_operand_ready")
        setup_mm = sem("setup_products")
        setup_ev = sem("setup_evacuated")
        setup_lo = sem("setup_low_parts")
        idx_rdy = sem("idx_float_ready")
        st_x = sem("x_stats")
        pow_rdy = sem("x_pow_done")
        x_steps = sem("x_stats_steps")
        h_rdy = sem("h_ready")
        hn_rdy = sem("hn_ready")
        n_rdy = sem("normed_ready")
        hnT_mm = sem("hn_transposed")
        cT_mm = sem("context_transposed")
        hnT_lo_rdy = sem("hnT_low_part")
        nT_ev = sem("normedT_ready")
        cT_ev = sem("contextT_ready")
        q_mm = sem("query_product")
        q_ev = sem("qT_ready")
        log_mm = sem("logits_product")
        log_rdy = sem("masked_logits_max")
        neg_rdy = sem("neg_max_ready")
        exp_rdy = sem("exp_done")
        pT_mm = sem("probs_transposed")
        pT_ev = sem("probsT_ready")
        gate_mm = sem("gate_product")
        gate_rdy = sem("gate_logit_ready")
        tanh_rdy = sem("tanh_done")
        pv_mm = sem("values_product")
        last_steps = sem("last_pair_steps")
        ri_rdy = sem("inverse_sum_ready")
        diff_rdy = sem("diff_ready")
        mix_rdy = sem("mixed_ready")
        xh_rdy = sem("x_plus_h_ready")
        x2_rdy = sem("x2_ready")
        st2 = sem("x2_stats")
        ve_rdy = sem("x2_var_eps_ready")
        rstd_rdy = sem("x2_rstd_ready")
        shift_rdy = sem("x2_shift_ready")
        xn_rdy = sem("xn2_ready")
        x2_out = [sem(f"x2_stored{s}") for s in range(2)]
        xn_out = [sem(f"xn2_stored{s}") for s in range(2)]
        whi_rdy = sem("w_hi_ready")
        wlo0_rdy = sem("expert0_w_lo_ready")
        wlo_rdy = sem("w_lo_ready")
        gidx_rdy = sem("gather_idx_ready")
        xg_in = [sem(f"rows_gathered{s}") for s in range(2)]
        first_rows_in = [sem(f"first_rows_gathered{t}") for t in range(NT)]
        acc_in = sem("sums_gathered")
        scat = sem("sums_scattered")
        xT_mm = sem("rows_transposed")
        xhi_rdy = sem("x_hi_ready")
        xlo_rdy = sem("x_lo_ready")
        up_mm = sem("up_product")
        g_rdy = sem("gelu_done")
        last_g_half = sem("last_gelu_first_half")
        last_glo_half = sem("last_g_lo_first_half")
        glo_rdy = sem("g_lo_ready")
        out_mm = sem("expert_output")
        accb_rdy = sem("bias_added_to_sums")
        new_rdy = sem("new_sums_ready")
        tot_rdy = sem("slot_totals")
        skip_rdy = sem("skip_ready")
        fac_rdy = sem("factor_ready")
        sidx_rdy = sem("scatter_idx_ready")

        waits_taken = sem("waits_taken")

        block = ctx.enter_context(nc.Block())

        def take_waits(eng):
            eng.sem_inc(waits_taken, 1)

        def each_item(eng, body):
            body(0, 0, 0)
            with eng.Fori(0, 3) as i:
                body(2 * i + 1, 1, i)
                body(2 * i + 2, 0, i + 1)
            body(LAST, 1, 3)

        def each_pair(eng, body):
            body(0, 0, 0)
            with eng.Fori(0, 2) as i:
                body(2 * i + 1, 1, i)
                body(2 * i + 2, 0, i + 1)
            body(LAST - 2, 1, 2)
            body(LAST - 1, 0, 3)
            body(LAST, 1, 3)

        def has_second_next(pair):
            return not isinstance(pair, int) or pair + 2 < NPAIR

        def steps_of(e):
            if is_first(e):
                return [(0, 0), (1, 0), (0, 1), (1, 1)] + [(f, None) for f in range(2, NF)]
            return [(f, None) for f in range(NF)]

        def steps_before(e):
            return 0 if is_first(e) else NF * e + 2

        def steps_until(e):
            return NF * e + NF + 2

        def side_work(e, j):
            if is_first(e):
                return {0: None, 1: 0, 2: None, 3: 1}.get(j, j - 2)
            return j

        def step_slots(half):
            return slice(0, C) if half is None else slice(half * C // 2, (half + 1) * C // 2)

        def step_tiles(half):
            return range(NT) if half is None else range(half * NT // 2, (half + 1) * NT // 2)

        def x_parts_before(e):
            return 0 if is_first(e) else KH * e + KH

        def is_first(item):
            return isinstance(item, int) and item == 0

        def is_last(item):
            return isinstance(item, int) and item == LAST

        def w_chunk(e, c):
            if c < KH:
                return W1[ds(e, 1), c * P:(c + 1) * P, :].rearrange("e p f -> p (e f)")
            t = NF // (NCH - KH)
            return W2[ds(e, 1), (c - KH) * t * P:(c - KH + 1) * t * P, :].rearrange("e (f p) d -> p (e f) d", p=P)

        def w_chunk_dst(c):
            dst = w_raw[:, c * CH:(c + 1) * CH]
            return dst if c < KH else dst.rearrange("p (f d) -> p f d", d=H)

        @block.sync
        def _(sp):
            x_v = x_in.rearrange("b s h -> s b h")
            c_v = ctx_in.rearrange("b s h -> s b h")

            def row_broadcast(dst, vec):
                n = vec.shape[0]
                return sp.dma_start(dst, vec.rearrange("(a h) -> a h", a=1).broadcast_to([P, n]))

            def load_x(g, b0, b1_):
                sp.dma_start(x3[:, b0:b1_, :], x_v[:, b0:b1_, :]).then_inc(x_in_s[g], 16)

            def load_ctx(p):
                sp.dma_start(cnat[:, p % 2, :, :], c_v[:, 2 * p:2 * p + 2, :]).then_inc(c_in_s[p % 2], 16)

            def load_weight(n, w, loaded):
                sp.dma_start(wts[:, n, :, :], w.rearrange("(k p) h -> p k h", p=P)).then_inc(loaded, 16)

            load_x(0, 0, 2)
            sp.dma_start(norm_wT[:, :], norm_w.rearrange("(k p) -> p k", p=P), allow_slow_non_contiguous=True)\
                .then_inc(nwT_in, 16)
            load_weight(0, q_w, wts_in)
            load_weight(1, k_w, wts_in)
            load_x(1, 2, 4)
            for n in range(2):
                row_broadcast(norm_w_bc[:, n * H:(n + 1) * H], norm_w).then_inc(bc_in, 16)
            load_ctx(0)
            load_weight(2, gate_w, gatew_in)
            row_broadcast(gate_b_bc[:, :], gate_b).then_inc(bc_in, 16)
            load_x(2, 4, 10)
            load_ctx(1)
            load_x(3, 10, NB)
            for c in range(NCH):
                sp.dma_start(w_chunk_dst(c), w_chunk(0, c)).then_inc(w_in[c], 16)
            sp.dma_start(bias_rows[:, :], b1.rearrange("e (f p) -> (e f) p", p=P)).then_inc(bias_in, 16)
            sp.dma_start(idx_all[:, :, :], top_idx.rearrange("(p t) e -> p t e", t=NT)).then_inc(idx_in, 16)
            sp.dma_start(rows_dram[:, H:ROW], comb_w).then_inc(comb_in, 16)
            out_v = out.rearrange("b s h -> s b h")
            rows_v = rows_dram.rearrange("(b s) r -> s b r", s=S)

            def load_lists(part):
                n = C * NE // IDX_PARTS
                row_broadcast(idx_rows[:, part * n:(part + 1) * n],
                              top_idx.rearrange("c e -> (c e)")[part * n:(part + 1) * n]).then_inc(idxrows_in, 16)

            load_lists(0)
            load_lists(1)
            sp.wait_ge(pv_mm, 1)
            load_ctx(2)
            for r in range(NPAIR):
                sp.wait_ge(x2_rdy, r + 1)
                sp.dma_start(out_v[:, 2 * r:2 * r + 2, :], x2[:, r % 2, :, :]).then_inc(x2_out[r % 2], 16)
                if r + 3 < NPAIR:
                    sp.wait_ge(pv_mm, r + 2)
                    load_ctx(r + 3)
                if r == LAST:
                    for b in range(2):
                        sp.wait_ge(xn_rdy, 2 * r + b + 1)
                        sp.dma_start(rows_v[:, 2 * r + b, 0:H], xn2[:, r % 2, b, :]).then_inc(xn_out[r % 2], 16)
                else:
                    sp.wait_ge(xn_rdy, 2 * r + 2)
                    sp.dma_start(rows_v[:, 2 * r:2 * r + 2, 0:H], xn2[:, r % 2, :, :]).then_inc(xn_out[r % 2], 16)
                if r + 2 < IDX_PARTS:
                    load_lists(r + 2)
                if r == NPAIR - 1:
                    for t in range(NT):
                        sp.wait_ge(first_rows_in[t], 16)
                if r % 2 == 1:
                    sp.wait_ge(wlo0_rdy, r + 1)
                    sp.dma_start(w_chunk_dst(r // 2), w_chunk(1, r // 2)).then_inc(w_in[r // 2], 16)
            sp.wait_ge(pv_mm, NPAIR)
            row_broadcast(b2_bc, b2.rearrange("e h -> (e h)")).then_inc(b2_in, 16)
            with sp.Fori(2, NE) as e:
                for c in range(NCH):
                    sp.wait_ge(wlo_rdy, 8 * e - 16 + 2 * c + 2)
                    sp.dma_start(w_chunk_dst(c), w_chunk(e, c)).then_inc(w_in[c], 16)

        @block.gpsimd
        def _(pool):
            g = nc.gpsimd
            g.memset(junk[:, :], 0.0).then_inc(warm_rdy, 1)
            g.memset(ident[:, :], 0.0).then_inc(consts, 1)
            g.memset(half_neg[:, :, :], -0.5).then_inc(consts, 1)
            g.memset(causal[:, :], 0.0).then_inc(consts, 1)
            pool.wait_ge(consts, 3)
            g.affine_select(out=ident[:, :], in_=ident[:, :], compare_op=ALU.not_equal, fill=1.0, base=0,
                            pattern=[[-1, P]], channel_multiplier=1).then_inc(ident_rdy, 1)
            g.affine_select(out=causal[:, 0:S], in_=causal[:, 0:S], compare_op=ALU.is_ge, fill=MASKED, base=0,
                            pattern=[[-1, S]], channel_multiplier=1).then_inc(ident_rdy, 1)

            def x_powers(b0, b1_, n):
                pool.wait_ge(st_x, n)
                g.tensor_tensor(pow_out[:, :, b0:b1_], pow_in[:, :, b0:b1_], half_neg[:, :, b0:b1_], ALU.pow)\
                    .then_inc(pow_rdy, 1)

            def normed_rows(p, s):
                pool.wait_ge(hn_rdy, 2 * p + 2)
                g.tensor_tensor(normed[:, s, :, :].rearrange("p b h -> p (b h)"),
                                hn[:, s, :, :].rearrange("p b h -> p (b h)"), norm_w_bc[:, :], ALU.mult)\
                    .then_inc(n_rdy, 1)

            x_powers(0, 2, 1)
            x_powers(2, 4, 2)
            pool.wait_ge(bc_in, 48)
            normed_rows(0, 0)

            def rstd(r, s):
                pool.wait_ge(ve_rdy, r + 1)
                g.tensor_tensor(rstd2[:, s, :], var_eps[:, s, :], half_neg[:, 0, 0:2], ALU.pow).then_inc(rstd_rdy, 1)

            def expert0_lo(p):
                pool.wait_ge(whi_rdy, p + 1)
                col = ds(p * PIECE, PIECE)
                g.tensor_tensor(w_lo[:, 0, col], w_raw[:, col], w_hi[:, 0, col].bitcast(F32), ALU.subtract)\
                    .then_inc(wlo0_rdy, 1)

            def attention(p, s, use):
                pool.wait_ge(h_rdy, 2 * p + 2)
                g.tensor_tensor(x_plus_h[:, s, :], x_all[:, ds(p * (2 * H), 2 * H)],
                                h[:, s, :, :].rearrange("p b h -> p (b h)"), ALU.add).then_inc(xh_rdy, 1)
                if is_first(p):
                    x_powers(4, 6, 3)
                    x_powers(6, 10, 3)
                if not is_last(p):
                    if not is_first(p):
                        pool.wait_ge(pv_mm, p)
                        take_waits(pool)
                    normed_rows(p + 1, 1 - s)
                if is_first(p):
                    x_powers(10, NB, 4)
                else:
                    rstd(p - 1, 1 - s)
                if not is_last(p):
                    expert0_lo(p)

            each_pair(pool, attention)

            def seen_tile(t):
                g.affine_select(out=seen[:, t, :], in_=seen[:, t, :], compare_op=ALU.is_ge, fill=DUP, base=-t,
                                pattern=[[1, C]], channel_multiplier=-NT).then_inc(seen_rdy, 1)

            pool.wait_ge(pv_mm, NPAIR)
            g.memset(seen, 1.0).then_inc(consts, 1)
            pool.wait_ge(consts, 4)
            for t in range(NT - 1):
                seen_tile(t)
            rstd(LAST, 1)
            seen_tile(NT - 1)
            expert0_lo(LAST)

            idx = bass.IndirectOffsetOnAxis
            flat = out.rearrange("b s h -> (b s) h")

            def gather_rows(s):
                take_waits(pool)
                for t in range(NT):
                    g.indirect_dma_start(xg[:, s, t, :], None, rows_dram, idx(gidx[:, s, t:t + 1].bitcast(U32), 0))\
                        .then_inc(xg_in[s], 16)

            def gather_sums(s):
                take_waits(pool)
                for t in range(NT):
                    g.indirect_dma_start(accg[:, t, :], None, flat, idx(gidx[:, s, t:t + 1].bitcast(U32), 0))\
                        .then_inc(acc_in, 16)

            def scatter_sums(e):
                for t in range(NT):
                    pool.wait_ge(new_rdy, NT * e + t + 1)
                    take_waits(pool)
                    g.indirect_dma_start(flat, idx(sidx[:, t:t + 1].bitcast(U32), 0), newrow[:, t, :], None,
                                         bounds_check=N - 1, oob_is_err=False).then_inc(scat, 16)

            pool.wait_ge(comb_in, 16)
            for s in range(2):
                pool.wait_ge(xn_out[s], 16 * (NPAIR // 2) + 16 + 16 * s)
                pool.wait_ge(x2_out[s], 16 * (NPAIR // 2) + 16)
            pool.wait_ge(gidx_rdy, 1)
            for t in range(NT):
                g.indirect_dma_start(xg[:, 0, t, :], None, rows_dram, idx(gidx[:, 0, t:t + 1].bitcast(U32), 0))\
                    .then_inc(first_rows_in[t], 16)

            def expert(e, s, use):
                if not is_last(e):
                    pool.wait_ge(gidx_rdy, e + 2)
                    gather_rows(1 - s)
                if not is_first(e):
                    scatter_sums(e - 1)
                    pool.wait_ge(scat, 16 * NT * e)
                gather_sums(s)

            each_item(pool, expert)
            scatter_sums(LAST)
            pool.wait_ge(scat, 16 * NT * NE)

        @block.scalar
        def _(act):
            a = nc.scalar
            for s in range(2):
                act.sem_inc(x2_out[s], 16)
                act.sem_inc(xn_out[s], 16)

            def normed_transposed(p, s):
                for k in range(KH):
                    a.activation(keysT[:, s, :, k, 0:S], ps_hnT[:, k, :, :], ACT.Copy, scale=norm_wT[:, k:k + 1])\
                        .then_inc(nT_ev, 1)

            def hn_transposed(p, s):
                act.wait_ge(hnT_mm, p + 1)
                a.copy(hnT_hi[:, s, :, :], ps_hnT.rearrange("p k b t -> p k (b t)"))

            def query(p):
                act.wait_ge(q_mm, p + 1)
                a.copy(qT[:, :, :], ps_q).then_inc(q_ev, 1)

            def context_transposed(p, s):
                act.wait_ge(cT_mm, p + 1)
                a.copy(keysT[:, s, :, :, S:2 * S].rearrange("p b k t -> p k b t"), ps_cT).then_inc(cT_ev, 1)

            def M_high(m):
                act.wait_ge(setup_mm, m + 1)
                a.activation(M_hi[:, m, :], ps_log[m], ACT.Copy, scale=norm_wT[:, m:m + 1]).then_inc(setup_ev, 1)

            act.wait_ge(warm_rdy, 1)
            a.activation(rinv[:, :], junk[:, 0:2], ACT.Copy, scale=1.0)
            act.wait_ge(nwT_in, 16)
            M_high(0)
            hn_transposed(0, 0)
            normed_transposed(0, 0)
            M_high(1)
            query(0)
            context_transposed(0, 0)
            act.wait_ge(setup_mm, 3)
            a.copy(gateT_hi[:, :, :], ps_gate).then_inc(setup_ev, 1)
            hn_transposed(1, 1)
            normed_transposed(1, 1)

            def normalised_x2(r, s, use):
                act.wait_ge(xn_out[s], 16 * use + 16)
                act.wait_ge(shift_rdy, r + 1)
                for b in range(2):
                    a.activation(xn2[:, s, b, :], x2[:, s, b, :], ACT.Identity, bias=shift2[:, s, b:b + 1],
                                 scale=rstd2[:, s, b:b + 1]).then_inc(xn_rdy, 1)

            def expert0_hi(p):
                col = ds(p * PIECE, PIECE)
                a.copy(w_hi[:, 0, col], w_raw[:, col]).then_inc(whi_rdy, 1)

            def attention(p, s, use):
                for b in range(2):
                    act.wait_ge(neg_rdy, 2 * p + b + 1)
                    a.activation(probs[:, b, :], probs[:, b, :], ACT.Exp, bias=neg_mx[:, b:b + 1], scale=SCALE,
                                 accum_out=rsum[:, b:b + 1]).then_inc(exp_rdy, 1)
                if has_second_next(p):
                    hn_transposed(p + 2, s)
                act.wait_ge(pT_mm, p + 1)
                a.copy(probsT, ps_pT).then_inc(pT_ev, 1)
                if has_second_next(p):
                    normed_transposed(p + 2, s)
                act.wait_ge(gate_rdy, 2 * p + 2)
                a.activation(gate_t, gate_t, ACT.Tanh, scale=0.5).then_inc(tanh_rdy, 1)
                if not is_last(p):
                    query(p + 1)
                    context_transposed(p + 1, 1 - s)
                if is_first(p):
                    for c in range(NCH):
                        act.wait_ge(w_in[c], 16)
                if not is_last(p):
                    expert0_hi(p)
                if not is_first(p):
                    normalised_x2(p - 1, 1 - s, use if s == 1 else use - 1)

            each_pair(act, attention)
            normalised_x2(LAST, 1, 3)
            expert0_hi(NPAIR - 1)
            act.wait_ge(setup_mm, 4)
            a.copy(biasT[:, :], banks[0][:, 0:NE * NF]).then_inc(setup_ev, 1)

            def x_hi_part(e, s):
                for k in range(KH):
                    act.wait_ge(xT_mm, x_parts_before(e) + k + 1)
                    a.copy(x_hi[:, s, k, :], ps_xT[k][:, :]).then_inc(xhi_rdy, 1)

            def first_x_hi(half):
                for k in range(KH):
                    act.wait_ge(xT_mm, KH * half + k + 1)
                    a.copy(x_hi[:, 0, k, step_slots(half)], ps_xT0[half][k]).then_inc(xhi_rdy, 1)

            a.activation(rinv[:, :], junk[:, 0:2], ACT.Gelu_apprx_tanh)
            first_x_hi(0)

            def expert(e, s, use):
                for j, (f, half) in enumerate(steps_of(e)):
                    c = step_slots(half)
                    act.wait_ge(up_mm, steps_before(e) + j + 1)
                    bias = biasT[:, ds(e * NF + f, 1)]
                    if is_last(e) and j == NF - 1:
                        for part in range(2):
                            c = step_slots(part)
                            a.activation(g32[:, j % 2, c], ps_up[j % 2][:, c], ACT.Gelu_apprx_tanh, bias=bias)
                            a.activation(g_hi[:, j % 2, c], ps_up[j % 2][:, c], ACT.Gelu_apprx_tanh, bias=bias)\
                                .then_inc(last_g_half if part == 0 else g_rdy, 1)
                        continue
                    a.activation(g32[:, j % 2, c], ps_up[j % 2][:, c], ACT.Gelu_apprx_tanh, bias=bias)
                    a.activation(g_hi[:, j % 2, c], ps_up[j % 2][:, c], ACT.Gelu_apprx_tanh, bias=bias)\
                        .then_inc(g_rdy, 1)
                    if is_first(e) and j == 1:
                        first_x_hi(1)
                    part = side_work(e, j)
                    if part is not None and not is_last(e):
                        if part % 2 == 0:
                            act.wait_ge(w_in[part // 2], 16 * e + 32)
                        col = slice(part * PIECE, (part + 1) * PIECE)
                        a.copy(w_hi[:, 1 - s, col], w_raw[:, col]).then_inc(whi_rdy, 1)
                        if part == 4:
                            x_hi_part(e + 1, 1 - s)

            each_item(act, expert)

        @block.vector
        def _(dve):
            v = nc.vector

            steps = [0]

            def x_stats(b0, b1_, group):
                dve.wait_ge(x_in_s[group], 16)
                for b in range(b0, b1_):
                    v.bn_stats(bn6[:, b, :], x3[:, b, :]).then_inc(x_steps, 1)
                steps[0] += b1_ - b0
                dve.wait_ge(x_steps, steps[0])
                for b in range(b0, b1_):
                    v.bn_aggr(mv[:, b, :], bn6[:, b, :]).then_inc(x_steps, 1)
                steps[0] += b1_ - b0

            def x_variances(b0, b1_):
                dve.wait_ge(x_steps, steps[0])
                v.tensor_scalar(pow_in[:, 0, b0:b1_], mv[:, b0:b1_, 1], LN_EPS, None, ALU.add)
                v.tensor_scalar(pow_in[:, 1, b0:b1_], mv[:, b0:b1_, 1], 1.0 + RMS_EPS, LN_EPS * RMS_EPS,
                                ALU.mult, ALU.add).then_inc(st_x, 1)

            def x_rms(b0, b1_, n):
                dve.wait_ge(pow_rdy, n)
                v.tensor_tensor(rms_t[:, b0:b1_], pow_in[:, 1, b0:b1_], pow_out[:, 1, b0:b1_], ALU.mult)\
                    .then_inc(x_steps, 1)
                steps[0] += 1
                dve.wait_ge(x_steps, steps[0])
                v.tensor_tensor(rms[:, b0:b1_], rms_t[:, b0:b1_], pow_out[:, 0, b0:b1_], ALU.mult)\
                    .then_inc(x_steps, 1)
                steps[0] += 1

            mvf = mv[:, :, :].rearrange("p b c -> p (b c)")

            def hn_rows(p, s):
                for b in range(2):
                    v.tensor_scalar(hn[:, s, b, :], x_all[:, ds((2 * p + b) * H, H)], mvf[:, ds(4 * p + 2 * b, 1)],
                                    pow_out[:, 1, ds(2 * p + b, 1)], ALU.subtract, ALU.mult).then_inc(hn_rdy, 1)

            def h_rows(p, s, reused=True):
                if reused:
                    dve.wait_ge(xh_rdy, p - 1)
                    dve.wait_ge(diff_rdy, 2 * p - 2)
                for b in range(2):
                    v.tensor_scalar(h[:, s, b, :], x_all[:, ds((2 * p + b) * H, H)], mvf[:, ds(4 * p + 2 * b, 1)],
                                    pow_out[:, 0, ds(2 * p + b, 1)], ALU.subtract, ALU.mult).then_inc(h_rdy, 1)

            def M_low(m):
                dve.wait_ge(setup_ev, m + 1)
                v.scalar_tensor_tensor(M_lo[:, m, :], ps_log[m], norm_wT[:, m:m + 1], M_hi[:, m, :].bitcast(F32),
                                       ALU.mult, ALU.subtract).then_inc(setup_lo, 1)

            def hnT_low(p, s):
                dve.wait_ge(nT_ev, 2 * p + 2)
                v.tensor_tensor(hnT_lo[:, s, :, :], ps_hnT.rearrange("p k b t -> p k (b t)"),
                                hnT_hi[:, s, :, :].bitcast(F32), ALU.subtract).then_inc(hnT_lo_rdy, 1)

            x_stats(0, 2, 0)
            x_variances(0, 2)
            dve.wait_ge(pow_rdy, 1)
            hn_rows(0, 0)
            x_stats(2, 4, 1)
            x_variances(2, 4)
            h_rows(0, 0, False)
            dve.wait_ge(bc_in, 48)
            dve.wait_ge(nwT_in, 16)
            M_low(0)
            hnT_low(0, 0)
            M_low(1)
            dve.wait_ge(pow_rdy, 2)
            hn_rows(1, 1)
            h_rows(1, 1, False)
            x_rms(0, 4, 2)
            x_stats(4, 10, 2)
            x_variances(4, 10)
            dve.wait_ge(ident_rdy, 2)
            dve.wait_ge(setup_ev, 3)
            v.tensor_tensor(gateT_lo[:, :, :], ps_gate, gateT_hi[:, :, :].bitcast(F32), ALU.subtract)\
                .then_inc(setup_lo, 1)

            def finish_diff(p, s):
                for b in range(2):
                    if b == 0:
                        dve.wait_ge(pv_mm, p + 1)
                        dve.wait_ge(ri_rdy, p + 1)
                    v.scalar_tensor_tensor(diff[:, b, :], ps_pv[:, b, :], rinv[:, b:b + 1], h[:, s, b, :],
                                           ALU.mult, ALU.subtract).then_inc(diff_rdy, 1)

            def mix(p):
                dve.wait_ge(tanh_rdy, p + 1)
                dve.wait_ge(diff_rdy, 2 * p + 2)
                d = diff[:, :, :].rearrange("p b h -> p (b h)")
                v.scalar_tensor_tensor(d, gate_t, 1.0, d, ALU.add, ALU.mult).then_inc(mix_rdy, 1)

            def residual(p, s, use):
                dve.wait_ge(mix_rdy, p + 1)
                dve.wait_ge(xh_rdy, p + 1)
                dve.wait_ge(x2_out[s], 16 * use + 16)
                v.scalar_tensor_tensor(x2[:, s, :, :].rearrange("p b h -> p (b h)"),
                                       diff[:, :, :].rearrange("p b h -> p (b h)"), 0.5, x_plus_h[:, s, :],
                                       ALU.mult, ALU.add).then_inc(x2_rdy, 1)

            def stats2(p, s):
                dve.wait_ge(x2_rdy, p + 1)
                for b in range(2):
                    v.bn_stats(bn6b[:, b, :], x2[:, s, b, :]).then_inc(st2, 1)

            def aggr2(p, s):
                for b in range(2):
                    dve.wait_ge(st2, 4 * p + b + 1)
                    take_waits(dve)
                    v.bn_aggr(mv2[:, s, b, :], bn6b[:, b, :]).then_inc(st2, 1)
                dve.wait_ge(st2, 4 * p + 4)
                v.tensor_scalar(var_eps[:, s, :], mv2[:, s, :, 1], LN_EPS, None, ALU.add).then_inc(ve_rdy, 1)

            def shift(r, s):
                dve.wait_ge(rstd_rdy, r + 1)
                v.scalar_tensor_tensor(shift2[:, s, :], mv2[:, s, :, 0], -1.0, rstd2[:, s, :], ALU.mult, ALU.mult)\
                    .then_inc(shift_rdy, 1)

            def attention(p, s, use):
                last_use = use if s == 1 else use - 1
                if not is_first(p):
                    if has_second_next(p):
                        dve.wait_ge(n_rdy, p + 1)
                        take_waits(dve)
                        hn_rows(p + 2, s)
                    finish_diff(p - 1, 1 - s)
                    dve.wait_ge(pT_mm, p)
                for b in range(2):
                    dve.wait_ge(log_mm, 2 * p + b + 1)
                    take_waits(dve)
                    v.tensor_tensor_reduce(out=probs[:, b, :], in0=ps_log[b], in1=causal[:, :], scale=1.0,
                                           scalar=-3.0e38, op0=ALU.add, op1=ALU.max, accum_out=mx[:, b:b + 1])\
                        .then_inc(log_rdy, 1)
                for b in range(2):
                    dve.wait_ge(log_rdy, 2 * p + b + 1)
                    v.tensor_scalar(neg_mx[:, b:b + 1], mx[:, b:b + 1], -SCALE, None, ALU.mult).then_inc(neg_rdy, 1)
                if not is_first(p):
                    mix(p - 1)
                    residual(p - 1, 1 - s, last_use)
                else:
                    hnT_low(1, 1)
                    dve.wait_ge(n_rdy, 1)
                    dve.wait_ge(pow_rdy, 3)
                    hn_rows(2, 0)
                if isinstance(p, int) and p == X_GROUPS[-1][0] // 2:
                    x_rms(10, NB, 5)
                dve.wait_ge(gate_mm, p + 1)
                if isinstance(p, int):
                    dve.wait_ge(x_steps, steps[0])
                if not is_first(p):
                    dve.wait_ge(mix_rdy, p)
                for b in range(2):
                    v.scalar_tensor_tensor(gate_t[:, b * H:(b + 1) * H], ps_gate[:, b, :], rms[:, ds(2 * p + b, 1)],
                                           gate_b_bc[:, :], ALU.mult, ALU.add).then_inc(gate_rdy, 1)
                if is_first(p):
                    x_stats(10, NB, 3)
                else:
                    stats2(p - 1, 1 - s)
                if has_second_next(p):
                    hnT_low(p + 2, s)
                if is_first(p):
                    x_variances(10, NB)
                else:
                    aggr2(p - 1, 1 - s)
                    if not is_last(p):
                        h_rows(p + 1, 1 - s)
                dve.wait_ge(exp_rdy, 2 * p + 2)
                v.reciprocal(rinv[:, :], rsum[:, :]).then_inc(ri_rdy, 1)
                if is_first(p):
                    x_rms(4, 10, 4)
                    dve.wait_ge(x_steps, steps[0])
                elif not is_last(p):
                    shift(p - 1, 1 - s)
                    dve.wait_ge(pow_rdy, 5)

            each_pair(dve, attention)
            dve.wait_ge(idx_in, 16)
            v.tensor_copy(idx_f[:, :], idx_all[:, :, :].rearrange("p t e -> p (t e)")).then_inc(idx_rdy, 1)
            v.tensor_copy(gidx[:, 0, :], idx_all[:, :, 0]).then_inc(gidx_rdy, 1)

            last_s = (NPAIR - 1) % 2

            def last_pair_diff(b):
                v.scalar_tensor_tensor(diff[:, b, :], ps_pv[:, b, :], rinv[:, b:b + 1], h[:, last_s, b, :],
                                       ALU.mult, ALU.subtract).then_inc(last_steps, 1)

            dve.wait_ge(mix_rdy, NPAIR - 1)
            dve.wait_ge(ri_rdy, NPAIR)
            dve.wait_ge(pv_mm, NPAIR)
            last_pair_diff(0)
            last_pair_diff(1)
            shift(NPAIR - 2, 1 - last_s)
            dve.wait_ge(tanh_rdy, NPAIR)
            for b in range(2):
                dve.wait_ge(last_steps, b + 1)
                v.scalar_tensor_tensor(diff[:, b, :], gate_t[:, b * H:(b + 1) * H], 1.0, diff[:, b, :],
                                       ALU.add, ALU.mult).then_inc(last_steps, 1)
            dve.wait_ge(xh_rdy, NPAIR)
            dve.wait_ge(x2_out[last_s], 16 * (NPAIR // 2))
            for b in range(2):
                dve.wait_ge(last_steps, b + 3)
                x2_half = v.scalar_tensor_tensor(x2[:, last_s, b, :], diff[:, b, :], 0.5,
                                                 x_plus_h[:, last_s, b * H:(b + 1) * H], ALU.mult, ALU.add)
                x2_half.then_inc(last_steps if b == 0 else x2_rdy, 1)
            for b in range(2):
                if b == 0:
                    dve.wait_ge(last_steps, 5)
                else:
                    dve.wait_ge(x2_rdy, NPAIR)
                v.bn_stats(bn6b[:, b, :], x2[:, last_s, b, :]).then_inc(st2, 1)
            aggr2(NPAIR - 1, last_s)
            shift(NPAIR - 1, last_s)

            def first_x_lo(half):
                for k in range(KH):
                    c = step_slots(half)
                    dve.wait_ge(xhi_rdy, KH * half + k + 1)
                    v.tensor_tensor(x_lo[:, 0, k, c], ps_xT0[half][k], x_hi[:, 0, k, c].bitcast(F32), ALU.subtract)\
                        .then_inc(xlo_rdy, 1)

            first_x_lo(0)

            def x_lo_part(e, s):
                for k in range(KH):
                    dve.wait_ge(xhi_rdy, x_parts_before(e) + k + 1)
                    v.tensor_tensor(x_lo[:, s, k, :], ps_xT[k][:, :], x_hi[:, s, k, :].bitcast(F32), ALU.subtract)\
                        .then_inc(xlo_rdy, 1)

            def add_bias(e, tiles):
                dve.wait_ge(acc_in, 16 * NT * (e + 1))
                dve.wait_ge(fac_rdy, e + 1)
                for t in tiles:
                    v.scalar_tensor_tensor(accg[:, t, :], b2_bc[:, ds(e * H, H)], factor[:, t:t + 1], accg[:, t, :],
                                           ALU.mult, ALU.add).then_inc(accb_rdy, 1)

            def new_sums(e, tiles):
                dve.wait_ge(accb_rdy, NT * e + NT)
                for t in tiles:
                    dve.wait_ge(out_mm, NT * e + t + 1)
                    v.scalar_tensor_tensor(newrow[:, t, :], ps_down[t], factor[:, t:t + 1],
                                           accg[:, t, :], ALU.mult, ALU.add).then_inc(new_rdy, 1)

            TOTALS_AT = (1, 2, 3, 4)
            rows_by_expert = idx_rows[:, :].rearrange("p (c e) -> p e c", e=NE)

            def slot_total(e, t):
                v.scalar_tensor_tensor(junk[:, :], rows_by_expert[:, ds(e, 1), :].rearrange("p a c -> p (a c)"),
                                       idx_f[:, ds(t * NE + e, 1)], seen[:, t, :], ALU.is_equal, ALU.mult,
                                       accum_out=total[:, t:t + 1]).then_inc(tot_rdy, 1)


            def expert(e, s, use):
                if not is_last(e):
                    if not is_first(e):
                        dve.wait_ge(acc_in, 16 * NT * e)
                    v.tensor_copy(gidx[:, 1 - s, :], idx_all[:, :, ds(e + 1, 1)].rearrange("p t a -> p (t a)"))\
                        .then_inc(gidx_rdy, 1)
                for j, (f, half) in enumerate(steps_of(e)):
                    c = step_slots(half)
                    if j == 0 and not is_first(e):
                        new_sums(e - 1, range(NT // 2))
                    if is_last(e) and j == NF - 1:
                        for part in range(2):
                            c = step_slots(part)
                            if part == 0:
                                dve.wait_ge(last_g_half, 1)
                            else:
                                dve.wait_ge(g_rdy, steps_until(e))
                            v.tensor_tensor(g_lo[:, j % 2, c], g32[:, j % 2, c], g_hi[:, j % 2, c].bitcast(F32),
                                            ALU.subtract).then_inc(last_glo_half if part == 0 else glo_rdy, 1)
                        continue
                    dve.wait_ge(g_rdy, steps_before(e) + j + 1)
                    v.tensor_tensor(g_lo[:, j % 2, c], g32[:, j % 2, c], g_hi[:, j % 2, c].bitcast(F32), ALU.subtract)\
                        .then_inc(glo_rdy, 1)
                    if j == 0 and not is_first(e):
                        new_sums(e - 1, range(NT // 2, NT))
                    if is_first(e) and j == 1:
                        first_x_lo(1)
                    part = side_work(e, j)
                    if part is None:
                        continue
                    if not is_last(e):
                        col = slice(part * PIECE, (part + 1) * PIECE)
                        dve.wait_ge(whi_rdy, 8 * e + 8 + part + 1)
                        v.tensor_tensor(w_lo[:, 1 - s, col], w_raw[:, col], w_hi[:, 1 - s, col].bitcast(F32),
                                        ALU.subtract).then_inc(wlo_rdy, 1)
                        if part == 5:
                            x_lo_part(e + 1, 1 - s)
                    if part in TOTALS_AT:
                        n = TOTALS_AT.index(part)
                        if is_first(e) and n == 0:
                            dve.wait_ge(idxrows_in, 16 * IDX_PARTS)
                            dve.wait_ge(idx_rdy, 1)
                            dve.wait_ge(seen_rdy, NT)
                        if not is_first(e):
                            dve.wait_ge(tot_rdy, NT * e + n)
                        elif n:
                            dve.wait_ge(tot_rdy, n)
                        slot_total(e, n)
                    if part == (NF - 3 if is_last(e) else NF - 2):
                        dve.wait_ge(tot_rdy, NT * e + NT)
                        v.tensor_tensor(factor[:, :], total[:, :],
                                        xg[:, s, :, ds(e + H, 1)].rearrange("p t a -> p (t a)"), ALU.mult)\
                            .then_inc(fac_rdy, 1)
                        v.tensor_scalar(skip_f[:, :], total[:, :], DUP, SKIP, ALU.is_ge, ALU.mult).then_inc(skip_rdy, 1)
                        dve.wait_ge(skip_rdy, e + 1)
                        if not is_first(e):
                            dve.wait_ge(scat, 16 * NT * e)
                        v.tensor_tensor(sidx[:, :], skip_f[:, :],
                                        idx_f[:, :].rearrange("p (t e) -> p t e", e=NE)[:, :, ds(e, 1)]
                                        .rearrange("p t a -> p (t a)"), ALU.add).then_inc(sidx_rdy, 1)
                        if is_first(e):
                            dve.wait_ge(b2_in, 16)
                        add_bias(e, range(NT) if is_last(e) else range(NT // 2))
                    if part == NF - 1 and not is_last(e):
                        add_bias(e, range(NT // 2, NT))

            each_item(dve, expert)
            dve.wait_ge(sidx_rdy, NE)
            new_sums(LAST, range(NT))

        @block.tensor
        def _(pe):
            t_ = nc.tensor

            def keep_warm(n):
                for _ in range(n):
                    t_.matmul(banks[5][:, :], junk[:, 0:P], junk[:, :], start=True, stop=True)

            pe.wait_ge(warm_rdy, 1)
            keep_warm(9)
            pe.wait_ge(wts_in, 32)
            pe.wait_ge(ident_rdy, 2)
            def M_rows(m):
                for k in range(KH):
                    last = t_.matmul(ps_log[m], wts[:, 0, k, m * P:(m + 1) * P], wts[:, 1, k, :],
                                     start=(k == 0), stop=(k == KH - 1))
                last.then_inc(setup_mm, 1)

            def hn_transposes(p, s):
                pe.wait_ge(hn_rdy, 2 * p + 2)
                if not is_first(p):
                    pe.wait_ge(hnT_lo_rdy, p)
                for k in range(KH):
                    for b in range(2):
                        last = t_.transpose(ps_hnT[:, k, b, :], hn[:, s, b, k * P:(k + 1) * P], ident[:, :])
                last.then_inc(hnT_mm, 1)

            def three_passes(dst, lhs_hi, lhs_lo, rhs_hi, rhs_lo, first, last_one):
                t_.matmul(dst, lhs_hi, rhs_hi, start=first, stop=False)
                t_.matmul(dst, lhs_hi, rhs_lo, start=False, stop=False)
                return t_.matmul(dst, lhs_lo, rhs_hi, start=False, stop=last_one)

            def context_transposes(p, s, use):
                pe.wait_ge(c_in_s[s], 16 * use + 16)
                for k in range(KH):
                    for b in range(2):
                        last = t_.transpose(ps_cT[:, k, b, :], cnat[:, s, b, k * P:(k + 1) * P], ident[:, :])
                last.then_inc(cT_mm, 1)

            def query(p, s):
                pe.wait_ge(hnT_lo_rdy, p + 1)
                for m in range(KH):
                    c = slice(m * P, (m + 1) * P)
                    for k in range(KH):
                        last = three_passes(ps_q[:, m, :], M_hi[:, k, c], M_lo[:, k, c], hnT_hi[:, s, k, :],
                                            hnT_lo[:, s, k, :], k == 0, k == KH - 1)
                last.then_inc(q_mm, 1)

            M_rows(0)
            hn_transposes(0, 0)
            M_rows(1)
            pe.wait_ge(setup_lo, 2)
            query(0, 0)
            context_transposes(0, 0, 0)
            pe.wait_ge(gatew_in, 16)
            for k in range(KH):
                for o in range(KH):
                    last = t_.transpose(ps_gate[:, k, o * P:(o + 1) * P], wts[:, 2, o, k * P:(k + 1) * P], ident[:, :])
            last.then_inc(setup_mm, 1)
            hn_transposes(1, 1)

            def attention(p, s, use):
                pe.wait_ge(q_ev, p + 1)
                pe.wait_ge(cT_ev, p + 1)
                for b in range(2):
                    if not is_first(p):
                        pe.wait_ge(log_rdy, 2 * p - 1 + b)
                    for k in range(KH):
                        last = t_.matmul(ps_log[b], qT[:, k, b * S:(b + 1) * S], keysT[:, s, b, k, :],
                                         start=(k == 0), stop=(k == KH - 1))
                    last.then_inc(log_mm, 1)
                if is_first(p):
                    pe.wait_ge(setup_lo, 3)
                else:
                    pe.wait_ge(gate_rdy, 2 * p)
                for b in range(2):
                    c = slice(b * S, (b + 1) * S)
                    for k in range(KH):
                        last = three_passes(ps_gate[:, b, :], hnT_hi[:, s, k, c], hnT_lo[:, s, k, c],
                                            gateT_hi[:, k, :], gateT_lo[:, k, :], k == 0, k == KH - 1)
                last.then_inc(gate_mm, 1)
                if has_second_next(p):
                    hn_transposes(p + 2, s)
                if not is_last(p):
                    context_transposes(p + 1, 1 - s, use if s == 0 else use + 1)
                pe.wait_ge(exp_rdy, 2 * p + 2)
                for b in range(2):
                    for j in range(2):
                        last = t_.transpose(ps_pT[:, b, j, :], probs[:, b, j * S:(j + 1) * S], ident[:, :])
                last.then_inc(pT_mm, 1)
                if not is_last(p):
                    query(p + 1, 1 - s)
                pe.wait_ge(pT_ev, p + 1)
                pe.wait_ge(n_rdy, p + 1)
                if not is_first(p):
                    pe.wait_ge(diff_rdy, 2 * p)
                for b in range(2):
                    for j in range(2):
                        values = normed if j == 0 else cnat
                        last = t_.matmul(ps_pv[:, b, :], probsT[:, b, j, :], values[:, s, b, :],
                                         start=(j == 0), stop=(j == 1))
                last.then_inc(pv_mm, 1)

            each_pair(pe, attention)
            pe.wait_ge(bias_in, 16)
            t_.transpose(banks[0][:, 0:NE * NF], bias_rows[:, :], ident[0:NE * NF, 0:NE * NF]).then_inc(setup_mm, 1)

            def rows_transposed(e, s, rounds):
                pe.wait_ge(xg_in[s], 16 * NT * rounds)
                pe.wait_ge(xlo_rdy, x_parts_before(e))
                for k in range(KH):
                    for t in range(NT):
                        last = t_.transpose(ps_xT[k][:, t * P:(t + 1) * P], xg[:, s, t, k * P:(k + 1) * P], ident[:, :])
                    last.then_inc(xT_mm, 1)

            def w_lo_wait(e, pieces):
                if is_first(e):
                    pe.wait_ge(wlo0_rdy, pieces)
                else:
                    pe.wait_ge(wlo_rdy, 8 * e - 8 + pieces)

            def up(e, s, j):
                f, half = steps_of(e)[j]
                cols = step_slots(half)
                if not (is_first(e) and j < 2):
                    pe.wait_ge(g_rdy, steps_before(e) + j - 1)
                dst = ps_up[j % 2][:, cols]
                if f == 0:
                    w_lo_wait(e, 4)
                    for k in range(KH):
                        c = slice(k * FF, k * FF + P)
                        pe.wait_ge(xhi_rdy, x_parts_before(e) + KH * (half or 0) + k + 1)
                        t_.matmul(dst, w_hi[:, s, c], x_hi[:, s, k, cols], start=(k == 0), stop=False)
                        t_.matmul(dst, w_lo[:, s, c], x_hi[:, s, k, cols], start=False, stop=False)
                    for k in range(KH):
                        pe.wait_ge(xlo_rdy, x_parts_before(e) + KH * (half or 0) + k + 1)
                        last = t_.matmul(dst, w_hi[:, s, k * FF:k * FF + P], x_lo[:, s, k, cols], start=False,
                                         stop=(k == KH - 1))
                    last.then_inc(up_mm, 1)
                    return
                for k in range(KH):
                    c = slice(k * FF + f * P, k * FF + (f + 1) * P)
                    last = three_passes(dst, w_hi[:, s, c], w_lo[:, s, c], x_hi[:, s, k, cols], x_lo[:, s, k, cols],
                                        k == 0, k == KH - 1)
                last.then_inc(up_mm, 1)

            def down(e, s, j):
                f, half = steps_of(e)[j]
                if f == 0:
                    w_lo_wait(e, 8)
                by_halves = is_last(e) and j == -1
                if by_halves:
                    pe.wait_ge(last_glo_half, 1)
                else:
                    pe.wait_ge(glo_rdy, steps_before(e) + j + 1 if j >= 0 else steps_until(e))
                for t in step_tiles(half):
                    if by_halves and t == NT // 2:
                        pe.wait_ge(glo_rdy, steps_until(e))
                    if f == 0 and not is_first(e):
                        pe.wait_ge(new_rdy, NT * e - NT + t + 1)
                    g = slice(t * P, (t + 1) * P)
                    c = slice(W1C + f * H, W1C + (f + 1) * H)
                    last = three_passes(ps_down[t], g_hi[:, j % 2, g], g_lo[:, j % 2, g], w_hi[:, s, c],
                                        w_lo[:, s, c], f == 0, f == NF - 1)
                    if f == NF - 1:
                        last.then_inc(out_mm, 1)

            for s in range(2):
                pe.wait_ge(xn_out[s], 16 * (NPAIR // 2) + 16 + 16 * s)
            keep_warm(8)
            for t in range(NT):
                pe.wait_ge(first_rows_in[t], 16)
                half, col = t // (NT // 2), t % (NT // 2) * P
                for k in range(KH):
                    last = t_.transpose(ps_xT0[half][k][:, col:col + P], xg[:, 0, t, k * P:(k + 1) * P], ident[:, :])
                    if t % (NT // 2) == NT // 2 - 1:
                        last.then_inc(xT_mm, 1)
                if t % 2 == 0:
                    keep_warm(2 - t // 2)
                if t == NT // 2 - 1:
                    up(0, 0, 0)
                    up(0, 0, 1)

            def expert(e, s, use):
                if not is_first(e):
                    up(e, s, 0)
                    down(e - 1, 1 - s, -1)
                    up(e, s, 1)
                down(e, s, 0)
                for j in range(2, len(steps_of(e))):
                    if side_work(e, j) == 4 and not is_last(e):
                        rows_transposed(e + 1, 1 - s, use + 1)
                    up(e, s, j)
                    down(e, s, j - 1)

            each_item(pe, expert)
            down(LAST, 1, -1)


_INS = ['x', 'ctx_1024', 'L0_xattn_q_w', 'L0_xattn_k_w', 'L0_xattn_norm_w', 'L0_xattn_gate_w', 'L0_xattn_gate_b',
        'L0_ffn_combine_weights', 'L0_ffn_top_idx', 'L0_ffn_W1', 'L0_ffn_b1', 'L0_ffn_W2', 'L0_ffn_b2']


def kernel(**inputs):
    import numpy as _np
    import concourse.bacc as _bacc
    from concourse import mybir as _mybir
    from concourse.bass_utils import run_bass_kernel_spmd as _run

    nc = _bacc.Bacc("TRN2", target_bir_lowering=False, num_devices=1)
    arrays, args = {}, []
    for name in _INS:
        a = _np.ascontiguousarray(inputs[name])
        arrays[f"in_{name}_dram"] = a
        args.append(nc.dram_tensor(f"in_{name}_dram", a.shape, _mybir.dt.from_np(a.dtype), kind="ExternalInput").ap())
    args.append(nc.dram_tensor("out_0_dram", inputs["x"].shape, _mybir.dt.float32, kind="ExternalOutput").ap())
    build_xattn_moe(nc, *args)
    r = _run(nc, [arrays], core_ids=[0])
    return r.results[0]["out_0_dram"]
```
